# Optimizing a Trainium2 kernel written in Bass

```python
import numpy as np
import jax
import jax.numpy as jnp

def _softmax(x, axis=-1):
    return jax.nn.softmax(x, axis=axis)

def _gelu(x):
    return jax.nn.gelu(x, approximate=True)

def _silu(x):
    return jax.nn.silu(x)

def _sigmoid(x):
    return jax.nn.sigmoid(x)

def _layernorm(x, axis=-1, eps=1e-05):
    m = jnp.mean(x, axis=axis, keepdims=True)
    v = jnp.var(x, axis=axis, keepdims=True)
    return (x - m) / jnp.sqrt(v + eps)

def _scatter_add(tgt, idx, src, axis=0):
    return tgt.at[idx].add(src)

def _segment_sum(src, seg, n):
    return jax.ops.segment_sum(src, seg, n)
kernel_name = 'mk_lm_tower_d1_tok_ids1024_r4_b3ecfa'

def setup_inputs(seed: int=0):
    np.random.seed(seed)
    _w = jnp.asarray

    def _rec_inputs():
        import jax
        import jax.numpy as jnp
        _rk = jax.random.key(seed)
        x = jax.random.randint(jax.random.fold_in(_rk, 1), (8, 1024), 0, 12564, jnp.int32)
        return x
    x = _rec_inputs()

    def _L0_tok_setup():
        import jax, jax.numpy as jnp
        import numpy as np
        VOCAB = 50257
        DIM = 256
        PADDING_IDX = 0
        key = jax.random.key(seed)
        k_w, k_ids = jax.random.split(key)
        weight = jax.random.normal(k_w, (VOCAB, DIM), dtype=jnp.float32)
        weight = weight.at[PADDING_IDX].set(0.0)
        input_ids = jax.random.randint(k_ids, (16, 512), 0, VOCAB, dtype=jnp.int64)
        return {'weight': weight, 'input_ids': input_ids}
    _L0_tok_all = _L0_tok_setup()
    _L0_tok_in = {k: v for k, v in _L0_tok_all.items() if k in ('weight',)}
    del _L0_tok_all

    def _L0_attn_setup():
        import jax, jax.numpy as jnp
        import numpy as np
        NUM_HEADS = 16
        SCALE = (256 // NUM_HEADS) ** (-0.5)
        key = jax.random.key(seed)
        k1, k2, k3, k4, k5 = jax.random.split(key, 5)
        L, N, E, inner = (512, 4, 256, 256)
        return {'query': jax.random.normal(k1, (L, N, E), dtype=jnp.float32), 'qkv_proj': jax.random.normal(k2, (3 * inner, E), dtype=jnp.float32) * 0.02, 'qkv_bias': jax.random.normal(k3, (3 * inner,), dtype=jnp.float32) * 0.02, 'out_proj': jax.random.normal(k4, (E, inner), dtype=jnp.float32) * 0.02, 'out_bias': jax.random.normal(k5, (E,), dtype=jnp.float32) * 0.02}
    _L0_attn_all = _L0_attn_setup()
    _L0_attn_in = {k: v for k, v in _L0_attn_all.items() if k in ('qkv_proj', 'qkv_bias', 'out_proj', 'out_bias')}
    del _L0_attn_all

    def _L0_ffn_setup():
        import jax, jax.numpy as jnp
        import numpy as np
        H = 256
        I = 128
        IS = 256
        E = 16
        G = 4
        TOPK_G = 2
        TOPK = 4
        SCALE = 2.5
        B, S = (2, 256)

        def _relu2(x):
            r = jax.nn.relu(x)
            return r * r

        def _route(scores, bias_corr):
            T = scores.shape[0]
            s_choice = scores + bias_corr
            gs = s_choice.reshape(T, G, E // G)
            group_scores = jnp.sum(jax.lax.top_k(gs, 2)[0], axis=-1)
            gidx = jax.lax.top_k(group_scores, TOPK_G)[1]
            gmask = jnp.sum(jax.nn.one_hot(gidx, G, dtype=scores.dtype), axis=1)
            smask = jnp.repeat(gmask, E // G, axis=1)
            masked = jnp.where(smask > 0, s_choice, 0.0)
            topk_idx = jax.lax.top_k(masked, TOPK)[1]
            topk_w = jnp.take_along_axis(scores, topk_idx, axis=1)
            topk_w = topk_w / (jnp.sum(topk_w, axis=-1, keepdims=True) + 1e-20)
            topk_w = topk_w * SCALE
            return (topk_idx, topk_w)
        key = jax.random.key(seed)
        ks = jax.random.split(key, 8)
        sd = 0.02
        return {'hidden_states': jax.random.normal(ks[0], (B, S, H), jnp.float32), 'Wg': jax.random.normal(ks[1], (E, H), jnp.float32) * sd, 'bias_corr': jax.random.normal(ks[2], (E,), jnp.float32) * 0.01, 'W1': jax.random.normal(ks[3], (E, I, H), jnp.float32) * sd, 'W2': jax.random.normal(ks[4], (E, H, I), jnp.float32) * sd, 'Ws1': jax.random.normal(ks[5], (IS, H), jnp.float32) * sd, 'Ws2': jax.random.normal(ks[6], (H, IS), jnp.float32) * sd}
    _L0_ffn_all = _L0_ffn_setup()
    _L0_ffn_in = {k: v for k, v in _L0_ffn_all.items() if k in ('Wg', 'bias_corr', 'W1', 'W2', 'Ws1', 'Ws2')}
    del _L0_ffn_all
    return {'x': x, 'L0_tok_weight': _L0_tok_in['weight'], 'L0_attn_qkv_proj': _L0_attn_in['qkv_proj'], 'L0_attn_qkv_bias': _L0_attn_in['qkv_bias'], 'L0_attn_out_proj': _L0_attn_in['out_proj'], 'L0_attn_out_bias': _L0_attn_in['out_bias'], 'L0_ffn_Wg': _L0_ffn_in['Wg'], 'L0_ffn_bias_corr': _L0_ffn_in['bias_corr'], 'L0_ffn_W1': _L0_ffn_in['W1'], 'L0_ffn_W2': _L0_ffn_in['W2'], 'L0_ffn_Ws1': _L0_ffn_in['Ws1'], 'L0_ffn_Ws2': _L0_ffn_in['Ws2']}

def reference(x, L0_tok_weight, L0_attn_qkv_proj, L0_attn_qkv_bias, L0_attn_out_proj, L0_attn_out_bias, L0_ffn_Wg, L0_ffn_bias_corr, L0_ffn_W1, L0_ffn_W2, L0_ffn_Ws1, L0_ffn_Ws2):
    import jax
    import jax.numpy as jnp

    def _L0_tok_ref(weight, input_ids):
        import jax, jax.numpy as jnp
        import numpy as np
        VOCAB = 50257
        DIM = 256
        PADDING_IDX = 0
        return jnp.take(weight, input_ids, axis=0)

    def _L0_attn_ref(query, qkv_proj, qkv_bias, out_proj, out_bias):
        import jax, jax.numpy as jnp
        import numpy as np
        NUM_HEADS = 16
        SCALE = (256 // NUM_HEADS) ** (-0.5)
        L, N, E = query.shape
        h = NUM_HEADS
        inner = qkv_proj.shape[0] // 3
        d = inner // h
        qkv = jnp.einsum('lne,fe->lnf', query, qkv_proj) + qkv_bias
        qkv = qkv.reshape(L, N, inner, 3)
        q, k, v = (qkv[..., 0], qkv[..., 1], qkv[..., 2])
        q = q.reshape(L, N * h, d).transpose(1, 0, 2)
        k = k.reshape(L, N * h, d).transpose(1, 0, 2)
        v = v.reshape(L, N * h, d).transpose(1, 0, 2)
        attn = SCALE * jnp.einsum('bld,bmd->blm', q, k)
        attn = jax.nn.softmax(attn, axis=-1)
        out = jnp.einsum('blm,bmd->bld', attn, v)
        out = out.transpose(1, 0, 2).reshape(L, N, inner)
        out = jnp.einsum('lni,ei->lne', out, out_proj) + out_bias
        return out

    def _L0_ffn_ref(hidden_states, Wg, bias_corr, W1, W2, Ws1, Ws2):
        import jax, jax.numpy as jnp
        import numpy as np
        H = 256
        I = 128
        IS = 256
        E = 16
        G = 4
        TOPK_G = 2
        TOPK = 4
        SCALE = 2.5
        B, S = (2, 256)

        def _relu2(x):
            r = jax.nn.relu(x)
            return r * r

        def _route(scores, bias_corr):
            T = scores.shape[0]
            s_choice = scores + bias_corr
            gs = s_choice.reshape(T, G, E // G)
            group_scores = jnp.sum(jax.lax.top_k(gs, 2)[0], axis=-1)
            gidx = jax.lax.top_k(group_scores, TOPK_G)[1]
            gmask = jnp.sum(jax.nn.one_hot(gidx, G, dtype=scores.dtype), axis=1)
            smask = jnp.repeat(gmask, E // G, axis=1)
            masked = jnp.where(smask > 0, s_choice, 0.0)
            topk_idx = jax.lax.top_k(masked, TOPK)[1]
            topk_w = jnp.take_along_axis(scores, topk_idx, axis=1)
            topk_w = topk_w / (jnp.sum(topk_w, axis=-1, keepdims=True) + 1e-20)
            topk_w = topk_w * SCALE
            return (topk_idx, topk_w)
        b, s, h = hidden_states.shape
        flat = hidden_states.reshape(-1, h)
        T = flat.shape[0]
        logits = flat.astype(jnp.float32) @ Wg.T
        scores = jax.nn.sigmoid(logits)
        topk_idx, topk_w = _route(scores, bias_corr)
        topk_w = topk_w.astype(hidden_states.dtype)
        cw = jnp.zeros((T, E), flat.dtype)
        cw = cw.at[jnp.arange(T)[:, None], topk_idx].add(topk_w)
        hid = _relu2(jnp.einsum('th,eih->eti', flat, W1))
        y = jnp.einsum('eti,ehi->eth', hid, W2)
        out = jnp.einsum('eth,te->th', y, cw)
        shared = _relu2(flat @ Ws1.T) @ Ws2.T
        return (out + shared).reshape(b, s, h)
    h = _L0_tok_ref(L0_tok_weight, x)
    h = h + _L0_attn_ref(_layernorm(h, axis=-1), L0_attn_qkv_proj, L0_attn_qkv_bias, L0_attn_out_proj, L0_attn_out_bias)
    h = h + _L0_ffn_ref(_layernorm(h, axis=-1), L0_ffn_Wg, L0_ffn_bias_corr, L0_ffn_W1, L0_ffn_W2, L0_ffn_Ws1, L0_ffn_Ws2)
    return h

_drawn_inputs = setup_inputs


def setup_inputs(seed=0):
    import zlib

    import numpy as np

    out = dict(_drawn_inputs(seed))
    spreads = {}
    factors = {'L0_attn_qkv_bias': 7.985, 'L0_attn_out_bias': 2.814, 'L0_ffn_bias_corr': 4.834}
    for name, (base, spread) in spreads.items():
        noise = np.random.default_rng([zlib.crc32(name.encode()), seed]).standard_normal(out[name].shape)
        drawn = base * np.exp(spread * noise) if base else spread * noise
        out[name] = jnp.asarray(drawn.astype(out[name].dtype))
    for name, factor in factors.items():
        out[name] = (out[name] * factor).astype(out[name].dtype)
    return out
```

```python
import concourse.bass as bass
from concourse import mybir
from contextlib import ExitStack


def lm_tower_layer(nc: bass.Bass, ids, table, wqkv_t, bqkv, wo_t, bo, wg_t, bias_corr,
                   w1_t, ws1_t, w2_t, ws2_t, out):
    f32 = mybir.dt.float32
    f32r = mybir.dt.float32r
    i32 = mybir.dt.int32
    ALU = mybir.AluOpType
    ACT = mybir.ActivationFunctionType
    X = mybir.AxisListType.X

    P = 128
    VOCAB, D = table.shape
    L, N = out.shape[0], out.shape[1]
    NH = 16
    DH = D // NH
    HH = P // DH
    KH = D // P
    NN = 64
    T = NN * L
    TT = T // P
    B = N // NN
    E = wg_t.shape[1] // KH
    SH = ws1_t.shape[1] // (KH * P)
    X_ALL = E + SH
    G = 4
    EG = E // G
    TOPK_G, TOPK, ROUTE_SCALE = 2, 4, 2.5
    EPS = 1e-5
    ATT_SCALE = float(DH) ** -0.5
    LP = L // 2
    SLOTS = KH * LP
    QN = 2
    QS = E // QN
    HALF = 2 * X_ALL

    def nth(blk, per, k):
        i, off = blk
        return off * per + k if i is None else i * (2 * per) + (off * per + k)

    def turn(blk, per):
        i, off = blk
        return (off // 2) * per if i is None else i * per + (off // 2) * per

    def after(blk, d):
        return (blk[0], blk[1] + d)

    def block_ds(blk):
        return bass.ds(nth(blk, 1, 0), 1)

    def wait(eng, sem, value):
        if not isinstance(value, int) or value > 0:
            eng.wait_ge(sem, value)

    def wait_apart(eng, sem, value):
        value = value if isinstance(value, int) else eng.snap(value)
        eng.wait_ge(sem, 1)
        wait(eng, sem, value)

    ctx = ExitStack()
    with ctx:
        def sb(name, shape, dt=f32):
            return ctx.enter_context(nc.sbuf_tensor(name, shape, dt))

        def pb(name, shape):
            return ctx.enter_context(nc.psum_tensor(name, shape, f32))

        def sem(name):
            return ctx.enter_context(nc.semaphore(name))

        W1 = [sb(f"w1_{p}", [P, KH, X_ALL, P], f32r) for p in ("hi", "lo")]
        W2 = [sb(f"w2_{p}", [P, X_ALL, D], f32r) for p in ("hi", "lo")]
        WQKV = [sb(f"wqkv_{p}", [P, KH, 6, P], f32r) for p in ("hi", "lo")]
        WO = [sb(f"wo_{p}", [P, KH, D], f32r) for p in ("hi", "lo")]
        WG = sb("wg_hi_lo", [P, KH, 2, E], f32r)
        ident = sb("ident", [P, P])
        head_sum = sb("head_sum", [P, 4, 32])
        spread = sb("spread", [P, KH * L, P], f32r)
        bq = sb("bqkv_sb", [P, 6])
        bo_sb = sb("bo_sb", [P, D])
        bc_sb = sb("bias_corr_sb", [P, E])
        half_neg = sb("half_neg", [P, TT])
        lower = sb("lower", [P, TT, G, G])
        not_first = sb("not_first", [P, TT, E])
        idx = sb("idx", [P, B * TT], i32)
        idx_now = sb("idx_now", [P, TT], i32)
        xin = [sb(f"xin{p}", [P, TT, D]) for p in range(2)]
        h1 = [sb(f"h1_{p}", [P, TT, D]) for p in range(2)]
        xT1 = [sb(f"xT1_{p}", [P, KH, T], f32r) for p in ("hi", "lo")]
        xT2 = [[sb(f"xT2_{p}{q}", [P, KH, T], f32r) for p in ("hi", "lo")] for q in range(2)]
        q_sb = sb("q_sb", [P, KH, T])
        k_sb = sb("k_sb", [P, KH, T])
        v_sb = sb("v_sb", [P, KH, T])
        ring = sb("ring", [P, 4, 2, T])
        s_sb = sb("s_sb", [P, L, NN])
        pr = [sb(f"probs_{p}", [P, T], f32r) for p in ("hi", "lo")]
        s_max = sb("s_max", [P, NN])
        s_sum = sb("s_sum", [P, NN])
        s_rec = sb("s_rec", [P, NN])
        stats = [sb(f"stats{w}", [P, TT, 6]) for w in range(2)]
        mv = [sb(f"mv{w}", [P, 3, TT]) for w in range(2)]
        veps = [sb(f"veps{w}", [P, TT]) for w in range(2)]
        rstd = [sb(f"rstd{w}", [P, TT]) for w in range(2)]
        lg = sb("lg", [P, TT, 2, E])
        lgt = sb("lgt", [P, TT, E])
        sig = sb("sig", [P, TT, E])
        cho = sb("cho", [P, TT, E])
        pairs = sb("pairs", [P, TT * G, 6])
        gsc = sb("gsc", [P, TT, G])
        g_gt = sb("g_gt", [P, TT, G, G])
        g_ge = sb("g_ge", [P, TT, G, G])
        g_rank = sb("g_rank", [P, TT * G])
        g_in = sb("g_in", [P, TT * G])
        top8 = sb("top8", [P, TT, 8])
        e_gt = sb("e_gt", [P, TT, E])
        e_eq = sb("e_eq", [P, TT, E])
        e_pre = sb("e_pre", [P, TT, E])
        n_gt = sb("n_gt", [P, TT])
        w_sum = sb("w_sum", [P, TT])
        w_rec = sb("w_rec", [P, TT])
        cw = sb("cw", [P, TT, E])
        cwT = sb("cwT", [E, T])
        cwB = sb("cwB", [P, 2, QN, T])
        stage = cwB[:, :, :, :].rearrange("p a b t -> p a (b t)")
        r_sb = sb("r_sb", [P, 2, T])
        p_sb = sb("p_sb", [P, 2, T])
        hid = [sb(f"hid_{p}", [P, 2, T], f32r) for p in ("hi", "lo")]

        psH = pb("psH", [P, 2, T])
        psY = pb("psY", [P, 2, T])
        psA = pb("psA", [P, 2, T])
        psB = pb("psB", [P, 2, T])

        cw_dram = nc.dram_tensor("cw_dram", (B, E * T), f32, kind="Internal").ap()

        idx_in = sem("idx_in")
        small_in = sem("small_in")
        w_in = [sem("w_in0"), sem("w_in1")]
        w_hi = sem("w_hi")
        w_lo = sem("w_lo")
        const_step = sem("const_step")
        spread_ready = sem("spread_ready")
        idx_now_ready = sem("idx_now_ready")
        xin_in = [sem("xin_in0"), sem("xin_in1")]
        ln_stats = [sem("ln1_stats"), sem("ln2_stats")]
        ln_aggr = [sem("ln1_aggr"), sem("ln2_aggr")]
        ln_rstd = [sem("ln1_rstd"), sem("ln2_rstd")]
        xn_ready = [sem("xn1_ready"), sem("xn2_ready")]
        xT_mm = [sem("xT1_mm"), sem("xT2_mm")]
        xT_hi = [sem("xT1_hi_ready"), sem("xT2_hi_ready")]
        xT_lo = [sem("xT1_lo_ready"), sem("xT2_lo_ready")]
        xb_ready = sem("xb_ready")
        qkv_mm = sem("qkv_mm")
        qkv_ready = sem("qkv_ready")
        prod_ready = sem("prod_ready")
        score_mm = sem("score_mm")
        smax_ready = sem("smax_ready")
        ssub_ready = sem("ssub_ready")
        exp_ready = sem("exp_ready")
        ssum_ready = sem("ssum_ready")
        probs_ready = sem("probs_ready")
        probs_hi = sem("probs_hi_ready")
        probs_lo = sem("probs_lo_ready")
        spread_mm = sem("spread_mm")
        av_ready = sem("av_ready")
        msum1 = sem("msum1")
        msum2 = sem("msum2")
        o_ready = sem("o_ready")
        o_hi = sem("o_hi_ready")
        o_lo = sem("o_lo_ready")
        outp_mm = sem("outp_mm")
        h1_ready = sem("h1_ready")
        logit_mm = sem("logit_mm")
        lg_ready = sem("lg_ready")
        route_step = sem("route_step")
        sigexp_ready = sem("sigexp_ready")
        cwT_mm = sem("cwT_mm")
        cwT_ready = sem("cwT_ready")
        cwT_stored = sem("cwT_stored")
        cwB_in = [sem("cwB_in0"), sem("cwB_in1")]
        h_mm = sem("h_mm")
        relu_done = sem("relu_done")
        sq_done = sem("sq_done")
        p_ready = sem("p_ready")
        hid_hi = sem("hid_hi_ready")
        hid_lo = sem("hid_lo_ready")
        w2_mm = sem("w2_mm")
        y_added = sem("y_added")
        out_stored = sem("out_stored")
        h1_free = sem("h1_free")
        CREDIT = 2
        ROUTE_STEPS = 30
        CONST_IDENT = 3
        CONST_ALL = 15

        def flat(t):
            return t[:, :, :, :].rearrange("p a b c -> p (a b c)") if len(t.shape) == 4 else \
                t[:, :, :].rearrange("p a b -> p (a b)")

        PIECES = []

        def cut(src, dst, base, total, step):
            for at in range(0, total, step):
                n = min(step, total - at)
                PIECES.append((src[:, at:at + n], n, [flat(d)[:, base + at:base + at + n] for d in dst]))

        cut(wqkv_t, WQKV, 0, KH * 6 * P, 768)
        PIECES_QKV = len(PIECES)
        cut(wo_t, WO, 0, KH * D, KH * D)
        for kh in range(KH):
            PIECES.append((wg_t[:, kh * E:(kh + 1) * E], E, [WG[:, kh, s, :] for s in range(2)]))
        PIECES_ATT = len(PIECES)
        for kh in range(KH):
            for src, first, n_e in ((ws1_t, 0, SH), (w1_t, SH, E)):
                cut(src[:, kh * n_e * P:(kh + 1) * n_e * P], W1, (kh * X_ALL + first) * P, n_e * P, 1024)
        cut(ws2_t, W2, 0, SH * D, 1024)
        cut(w2_t, W2, SH * D, E * D, 1024)
        PIECES_ALL = len(PIECES)

        QKV_ORDER = [(0, 0), (1, 0), (0, 1), (1, 1), (2, 0), (2, 1)]
        QKV_SB = [q_sb, k_sb, v_sb]

        block = ctx.enter_context(nc.Block())

        @block.sync
        def _(sp):
            sp.sem_inc(h1_free, 2)
            sp.dma_start(idx[:, :], ids).then_inc(idx_in, 16)
            sp.dma_start(bq[:, :], bqkv).then_inc(small_in, 16)
            sp.dma_start(bo_sb[:, :], bo.partition_broadcast(P)).then_inc(small_in, 16)
            sp.dma_start(bc_sb[:, :], bias_corr.partition_broadcast(P)).then_inc(small_in, 16)
            for k, (src, n, _dst) in enumerate(PIECES):
                if k >= 2:
                    sp.wait_ge(w_lo, k - 1)
                sp.dma_start(stage[:, k % 2, 0:n], src).then_inc(w_in[k % 2], 16)
            sp.wait_ge(w_lo, PIECES_ALL)

            out_v = out.rearrange("(j q) (b n) d -> q b n j d", q=2, n=NN)

            def block_io(blk):
                sp.wait_ge(cwT_ready, nth(blk, 1, 1))
                sp.dma_start(cw_dram[block_ds(blk), :].rearrange("o (e t) -> (o e) t", t=T),
                             cwT[:, :]).then_inc(cwT_stored, 16)
                sp.wait_ge(cwT_stored, nth(blk, 16, 16))
                for g in range(QS):
                    if g >= 2:
                        sp.wait_ge(p_ready, nth(blk, E, QN * (g - 1)))
                    src = cw_dram[block_ds(blk), g * QN * T:(g + 1) * QN * T]
                    sp.dma_start(cwB[:, g % 2, :, :].rearrange("p a t -> p (a t)"),
                                 src.partition_broadcast(P)).then_inc(cwB_in[g % 2], 16)
                sp.wait_ge(y_added, nth(blk, 1, 2))
                par = blk[1] % 2
                for q in range(2):
                    sp.dma_start(out_v[q, block_ds(blk), :, :, :].rearrange("o n j d -> (o n) j d"),
                                 h1[par][q * NN:(q + 1) * NN, :, :]).then_inc(out_stored, 16)
                sp.wait_ge(out_stored, nth(blk, 32, 32))
                sp.sem_inc(h1_free, 1)

            with sp.Fori(0, B // 2) as i:
                block_io((i, 0))
                block_io((i, 1))

        @block.gpsimd
        def _(pool):
            steps = [0]

            def link(ins):
                steps[0] += 1
                ins.then_inc(const_step, 1)
                pool.wait_ge(const_step, steps[0])

            def gather(blk):
                wait(pool, h1_ready, nth(blk, 1, -1))
                nc.gpsimd.tensor_copy(idx_now[:, :], idx[:, bass.ds(nth(blk, TT, 0), TT)]).then_inc(idx_now_ready, 1)
                wait_apart(pool, idx_now_ready, nth(blk, 1, 1) - 2)
                par = blk[1] % 2
                for j in range(TT):
                    nc.gpsimd.indirect_dma_start(xin[par][:, j, :], None, table,
                                                 bass.IndirectOffsetOnAxis(idx_now[:, j:j + 1], 0)
                                                 ).then_inc(xin_in[par], 16)

            def gather_first(b):
                for j in range(TT):
                    nc.gpsimd.indirect_dma_start(xin[b][:, j, :], None, table,
                                                 bass.IndirectOffsetOnAxis(idx[:, b * TT + j:b * TT + j + 1], 0)
                                                 ).then_inc(xin_in[b], 16)

            def rstd_of(w, blk):
                pool.wait_ge(ln_aggr[w], nth(blk, 1, 1))
                nc.gpsimd.tensor_tensor(rstd[w][:, :], veps[w][:, :], half_neg[:, :], ALU.pow).then_inc(ln_rstd[w], 1)

            def position_sum(blk, t):
                a = ring[:, t % 4, :, :].rearrange("p l (m n) -> p l m n", m=L)
                ih, lp = t // LP, t % LP
                pool.wait_ge(av_ready, nth(blk, SLOTS, t + 1))
                nc.gpsimd.tensor_tensor(a[:, :, 0:4, :], a[:, :, 0:4, :], a[:, :, 4:8, :], ALU.add).then_inc(msum1, 1)
                pool.wait_ge(msum1, nth(blk, SLOTS, t + 1))
                nc.gpsimd.tensor_tensor(a[:, :, 0:2, :], a[:, :, 0:2, :], a[:, :, 2:4, :], ALU.add).then_inc(msum2, 1)
                pool.wait_ge(msum2, nth(blk, SLOTS, t + 1))
                o = q_sb[:, ih, 2 * lp * NN:(2 * lp + 2) * NN].rearrange("p (l n) -> p l n", l=2)
                nc.gpsimd.tensor_tensor(o, a[:, :, 0, :], a[:, :, 1, :], ALU.add).then_inc(o_ready, 1)

            def head(blk):
                rstd_of(0, blk)
                pool.wait_ge(xn_ready[0], nth(blk, 1, 1))
                par = blk[1] % 2
                nc.gpsimd.tensor_tensor(xin[par][:, :, :], xin[par][:, :, :],
                                        bo_sb[:, :].unsqueeze(1).to_broadcast([P, TT, D]), ALU.add).then_inc(xb_ready, 1)

            def main(blk):
                for t in range(SLOTS):
                    position_sum(blk, t)
                rstd_of(1, blk)

            pool.wait_ge(idx_in, 16)
            gather_first(0)
            link(nc.gpsimd.memset(half_neg[:, :], -0.5))
            link(nc.gpsimd.memset(ident[:, :], 0.0))
            link(nc.gpsimd.affine_select(out=ident[:, :], in_=ident[:, :], compare_op=ALU.not_equal, fill=1.0,
                                         base=0, pattern=[[-1, P]], channel_multiplier=1))
            gather_first(1)
            pool.wait_ge(small_in, 48)
            head((None, 0))
            link(nc.gpsimd.memset(head_sum[:, :, :], 1.0))
            link(nc.gpsimd.affine_select(out=head_sum[:, :, :], in_=head_sum[:, :, :], compare_op=ALU.is_ge, fill=0.0,
                                         base=0, pattern=[[P, 4], [-DH, 32]], channel_multiplier=1))
            link(nc.gpsimd.affine_select(out=head_sum[:, :, :], in_=head_sum[:, :, :], compare_op=ALU.is_ge, fill=0.0,
                                         base=DH - 1, pattern=[[-P, 4], [DH, 32]], channel_multiplier=-1))
            sp_f = ring[:, 0:2, :, :].rearrange("p a b c -> p (a b c)")
            link(nc.gpsimd.memset(sp_f, 0.0))
            for ih in range(KH):
                v = sp_f[:, ih * L * P:(ih + 1) * L * P].rearrange("p (a b h d) -> p a b h d", a=LP, b=2, h=HH)
                for b in range(2):
                    link(nc.gpsimd.affine_select(out=v[:, :, b, :, :], in_=v[:, :, b, :, :], compare_op=ALU.not_equal,
                                                 fill=1.0, base=-(64 * ih + 32 * b), channel_multiplier=1,
                                                 pattern=[[-HH, LP], [-1, HH], [0, DH]]))
            link(nc.gpsimd.memset(lower[:, :, :, :], 1.0))
            link(nc.gpsimd.affine_select(out=lower[:, :, :, :], in_=lower[:, :, :, :], compare_op=ALU.is_gt, fill=0.0,
                                         base=0, pattern=[[0, TT], [1, G], [-1, G]], channel_multiplier=0))
            link(nc.gpsimd.memset(not_first[:, :, :], 1.0))
            link(nc.gpsimd.affine_select(out=not_first[:, :, :], in_=not_first[:, :, :], compare_op=ALU.is_gt,
                                         fill=0.0, base=0, pattern=[[0, TT], [1, E]], channel_multiplier=0))
            assert steps[0] == CONST_ALL
            main((None, 0))
            head((None, 1))

            def block_pool(blk):
                gather(after(blk, 2))
                main(after(blk, 1))
                head(after(blk, 2))

            with pool.Fori(0, B // 2 - 1) as i:
                block_pool((i, 0))
                block_pool((i, 1))
            main((None, B - 1))

        @block.scalar
        def _(act):
            act.sem_inc(relu_done, CREDIT)
            act.sem_inc(hid_hi, CREDIT)

            def weight_hi(k):
                src, n, dst = PIECES[k]
                act.wait_ge(w_in[k % 2], 16 * (k // 2 + 1))
                nc.scalar.copy(dst[0], stage[:, k % 2, 0:n]).then_inc(w_hi, 1)

            def relu_square(blk, e):
                act.wait_ge(h_mm, nth(blk, X_ALL, e + 1))
                act.wait_ge(hid_lo, nth(blk, X_ALL, e + 1))
                nc.scalar.activation(r_sb[:, e % 2, :], psH[:, e % 2, :], ACT.Relu).then_inc(relu_done, 1)
                act.wait_ge(relu_done, nth(blk, X_ALL, e + 1 + CREDIT))
                nc.scalar.activation(r_sb[:, e % 2, :], r_sb[:, e % 2, :], ACT.Square).then_inc(sq_done, 1)

            def hidden_hi(blk, e):
                if e < SH:
                    act.wait_ge(sq_done, nth(blk, X_ALL, e + 1))
                    src = r_sb
                else:
                    act.wait_ge(p_ready, nth(blk, E, e - SH + 1))
                    src = p_sb
                act.wait_ge(w2_mm, nth(blk, X_ALL, e + 1))
                nc.scalar.copy(hid[0][:, e % 2, :], src[:, e % 2, :]).then_inc(hid_hi, 1)

            def transposed_hi(w, blk):
                act.wait_ge(xT_mm[w], nth(blk, 1, 1))
                if w == 0:
                    wait(act, outp_mm, nth(blk, 1, 0))
                    dst, src = xT1[0], psA
                else:
                    dst, src = xT2[blk[1] % 2][0], psB
                nc.scalar.copy(dst[:, :, :], src[:, :, :]).then_inc(xT_hi[w], 1)

            def qkv_out(blk, n):
                c, ih = QKV_ORDER[n]
                act.wait_ge(qkv_mm, nth(blk, 6, n + 1))
                if n == 0:
                    wait(act, o_lo, nth(blk, 2, 0))
                nc.scalar.activation(QKV_SB[c][:, ih, :], psB[:, n % 2, :], ACT.Identity,
                                     bias=bq[:, 2 * c + ih:2 * c + ih + 1]).then_inc(qkv_ready, 1)

            def attention(blk, h):
                if h == 0:
                    qkv_out(blk, 0)
                    qkv_out(blk, 1)
                elif h == 1:
                    qkv_out(blk, 2)
                    qkv_out(blk, 3)
                elif h in (2, 3):
                    qkv_out(blk, h + 2)
                elif h == 8:
                    act.wait_ge(ssub_ready, nth(blk, 1, 1))
                    nc.scalar.activation(s_sb[:, :, :], s_sb[:, :, :], ACT.Exp, scale=ATT_SCALE).then_inc(exp_ready, 1)
                elif h == 10:
                    act.wait_ge(probs_ready, nth(blk, 1, 1))
                    wait(act, spread_mm, nth(blk, SLOTS, 0))
                    nc.scalar.copy(pr[0][:, :], s_sb[:, :, :].rearrange("p m n -> p (m n)")).then_inc(probs_hi, 1)
                elif h in (17, 21):
                    ih = 0 if h == 17 else 1
                    act.wait_ge(o_ready, nth(blk, SLOTS, LP * (ih + 1)))
                    act.wait_ge(qkv_mm, nth(blk, 6, 6))
                    nc.scalar.copy(xT1[0][:, ih, :], q_sb[:, ih, :]).then_inc(o_hi, 1)
                elif h == 27:
                    transposed_hi(1, blk)
                elif h == 30:
                    act.wait_ge(logit_mm, nth(blk, 1, 1))
                    wait(act, route_step, nth(blk, ROUTE_STEPS, 1 - ROUTE_STEPS))
                    nc.scalar.copy(lg[:, :, :, :].rearrange("p a b c -> p (a b c)"),
                                   psA[:, 0, 0:TT * 2 * E]).then_inc(lg_ready, 1)
                elif h == 31:
                    act.wait_ge(route_step, nth(blk, ROUTE_STEPS, 1))
                    nc.scalar.activation(sig[:, :, :], lgt[:, :, :], ACT.Exp, scale=-1.0).then_inc(sigexp_ready, 1)

            def head(blk, h):
                if h == 28:
                    transposed_hi(0, blk)

            def weights_out(blk):
                act.wait_ge(cwT_mm, nth(blk, 1, 1))
                nc.scalar.copy(cwT[:, :], psA[0:E, 1, :]).then_inc(cwT_ready, 1)

            def block_act(blk, att, nxt):
                for e in range(X_ALL):
                    if e + 1 < X_ALL:
                        relu_square(blk, e + 1)
                    elif att is not None:
                        relu_square(att, 0)
                    for h, last in ((2 * e, False), (2 * e + 1, True)):
                        if att is not None:
                            attention(att, h)
                        if nxt is not None:
                            head(nxt, h)
                        if last:
                            break
                        if e == 0:
                            weights_out(blk)
                        if e + 1 < X_ALL:
                            hidden_hi(blk, e + 1)
                        elif att is not None:
                            hidden_hi(att, 0)

            for k in range(PIECES_QKV):
                weight_hi(k)
            act.wait_ge(const_step, CONST_IDENT)
            head((None, 0), 28)
            for k in range(PIECES_QKV, PIECES_ATT):
                weight_hi(k)
            act.wait_ge(const_step, CONST_ALL)
            nc.scalar.copy(spread[:, :, :].rearrange("p a b -> p (a b)"),
                           ring[:, 0:2, :, :].rearrange("p a b c -> p (a b c)")).then_inc(spread_ready, 1)
            act.wait_ge(small_in, 48)
            k = PIECES_ATT
            for h in range(HALF):
                attention((None, 0), h)
                if h >= 3 and k < PIECES_ALL:
                    weight_hi(k)
                    k += 1
                head((None, 1), h)
            assert k == PIECES_ALL
            relu_square((None, 0), 0)
            hidden_hi((None, 0), 0)
            with act.Fori(0, B // 2 - 1) as i:
                block_act((i, 0), (i, 1), (i, 2))
                block_act((i, 1), (i, 2), (i, 3))
            block_act((None, B - 2), (None, B - 1), None)
            block_act((None, B - 1), None, None)

        @block.vector
        def _(dve):
            dve.sem_inc(hid_lo, CREDIT)
            dve.sem_inc(y_added, 1)

            def weight_lo(k):
                src, n, dst = PIECES[k]
                dve.wait_ge(w_hi, k + 1)
                nc.vector.tensor_tensor(dst[1], stage[:, k % 2, 0:n], dst[0].bitcast(f32), ALU.subtract).then_inc(w_lo, 1)

            def weigh(blk, e):
                if e < SH:
                    return
                r = e - SH
                dve.wait_ge(sq_done, nth(blk, X_ALL, e + 1))
                if r % QN == 0:
                    g = r // QN
                    dve.wait_ge(cwB_in[g % 2], nth(blk, 16 * QS // 2, 16 * (g // 2 + 1)))
                dve.wait_ge(hid_hi, nth(blk, X_ALL, e + 1))
                nc.vector.tensor_tensor(p_sb[:, e % 2, :], r_sb[:, e % 2, :],
                                        cwB[:, (r // QN) % 2, r % QN, :], ALU.mult).then_inc(p_ready, 1)

            def hidden_lo(blk, e):
                src = r_sb if e < SH else p_sb
                dve.wait_ge(hid_hi, nth(blk, X_ALL, e + 1 + CREDIT))
                nc.vector.tensor_tensor(hid[1][:, e % 2, :], src[:, e % 2, :],
                                        hid[0][:, e % 2, :].bitcast(f32), ALU.subtract).then_inc(hid_lo, 1)

            def add_experts(blk):
                par = blk[1] % 2
                dve.wait_ge(w2_mm, nth(blk, X_ALL, X_ALL + CREDIT))
                nc.vector.tensor_tensor(h1[par][:, :, :].rearrange("p j d -> p (j d)"),
                                        psY[:, :, :].rearrange("p a t -> p (a t)"),
                                        h1[par][:, :, :].rearrange("p j d -> p (j d)"), ALU.add).then_inc(y_added, 1)

            def norm_stats(w, blk, src):
                for j in range(TT):
                    last = nc.vector.bn_stats(stats[w][:, j, :], src[:, j, :])
                last.then_inc(ln_stats[w], 1)
                dve.wait_ge(ln_stats[w], nth(blk, 3, 1))
                st, m = stats[w], mv[w]
                nc.vector.tensor_tensor(m[:, 0, :], st[:, :, 1], st[:, :, 4], ALU.add)
                nc.vector.tensor_tensor(m[:, 1, :], st[:, :, 1], st[:, :, 4], ALU.subtract)
                nc.vector.tensor_tensor(m[:, 2, :], st[:, :, 2], st[:, :, 5], ALU.add).then_inc(ln_stats[w], 1)
                dve.wait_ge(ln_stats[w], nth(blk, 3, 2))
                nc.vector.tensor_tensor(m[:, 1, :], m[:, 1, :], m[:, 1, :], ALU.mult)
                nc.vector.tensor_scalar(m[:, 0, :], m[:, 0, :], 0.5, None, ALU.mult)
                nc.vector.tensor_scalar(m[:, 2, :], m[:, 2, :], 1.0 / D, EPS, ALU.mult, ALU.add).then_inc(ln_stats[w], 1)
                dve.wait_ge(ln_stats[w], nth(blk, 3, 3))
                nc.vector.scalar_tensor_tensor(veps[w][:, :], m[:, 1, :], 0.25, m[:, 2, :], ALU.mult, ALU.add
                                               ).then_inc(ln_aggr[w], 1)

            def normalise(w, blk, src, dst):
                dve.wait_ge(ln_rstd[w], nth(blk, 1, 1))
                d = dst[:, :, :].rearrange("p a t -> p (a t)").rearrange("p (j d) -> p j d", d=D)
                for j in range(TT):
                    last = nc.vector.tensor_scalar(d[:, j, :], src[:, j, :], mv[w][:, 0, j:j + 1], rstd[w][:, j:j + 1],
                                                   ALU.subtract, ALU.mult)
                last.then_inc(xn_ready[w], 1)

            def transposed_lo(w, blk):
                src, dst = (psA, xT1) if w == 0 else (psB, xT2[blk[1] % 2])
                dve.wait_ge(xT_hi[w], nth(blk, 1, 1))
                nc.vector.tensor_tensor(dst[1][:, :, :], src[:, :, :], dst[0][:, :, :].bitcast(f32),
                                        ALU.subtract).then_inc(xT_lo[w], 1)

            def product(blk, t):
                lp, ih = t // KH, t % KH
                if t == 0:
                    dve.wait_ge(qkv_ready, nth(blk, 6, 2))
                elif t == 1:
                    dve.wait_ge(qkv_ready, nth(blk, 6, 4))
                if t < 4:
                    wait(dve, o_ready, nth(blk, SLOTS, t + 5 - SLOTS))
                else:
                    dve.wait_ge(score_mm, nth(blk, SLOTS, t - 3))
                qv = q_sb[:, ih, 2 * lp * NN:(2 * lp + 2) * NN].rearrange("p (l n) -> p l n", l=2)
                kv = k_sb[:, ih, :].rearrange("p (m n) -> p m n", m=L)
                nc.vector.tensor_tensor(ring[:, t % 4, :, :].rearrange("p l (m n) -> p l m n", m=L),
                                        qv.unsqueeze(2).to_broadcast([P, 2, L, NN]),
                                        kv.unsqueeze(1).to_broadcast([P, 2, L, NN]), ALU.mult).then_inc(prod_ready, 1)

            def weighted_values(blk, t):
                ih = t // LP
                dve.wait_ge(spread_mm, nth(blk, SLOTS, t + 1))
                if t == 0:
                    dve.wait_ge(qkv_ready, nth(blk, 6, 6))
                if t >= 4:
                    dve.wait_ge(o_ready, nth(blk, SLOTS, t - 3))
                ps = psB if t % 2 == 0 else psA
                nc.vector.tensor_tensor(ring[:, t % 4, :, :], ps[:, :, :],
                                        v_sb[:, ih, :].unsqueeze(1).to_broadcast([P, 2, T]), ALU.mult
                                        ).then_inc(av_ready, 1)

            def route(blk, part):
                base = {0: 0, 1: 1, 2: 17}[part]
                done = [base]

                def link(ins):
                    done[0] += 1
                    ins.then_inc(route_step, 1)
                    dve.wait_ge(route_step, nth(blk, ROUTE_STEPS, done[0]))

                def step(ins):
                    done[0] += 1
                    ins.then_inc(route_step, 1)

                tt = nc.vector.tensor_tensor
                if part == 0:
                    dve.wait_ge(lg_ready, nth(blk, 1, 1))
                    step(tt(lgt[:, :, :], lg[:, :, 0, :], lg[:, :, 1, :], ALU.add))
                elif part == 1:
                    dve.wait_ge(sigexp_ready, nth(blk, 1, 1))
                    link(nc.vector.tensor_scalar_add(sig[:, :, :], sig[:, :, :], 1.0))
                    link(nc.vector.reciprocal(sig[:, :, :], sig[:, :, :]))
                    link(tt(cho[:, :, :], sig[:, :, :], bc_sb[:, :].unsqueeze(1).to_broadcast([P, TT, E]), ALU.add))
                    c4 = cho[:, :, :].rearrange("p t (g x) -> p (t g) x", x=EG)
                    step(tt(pairs[:, :, 0:3], c4[:, :, 0:3], c4[:, :, 1:4], ALU.add))
                    step(tt(pairs[:, :, 3:5], c4[:, :, 0:2], c4[:, :, 2:4], ALU.add))
                    link(tt(pairs[:, :, 5:6], c4[:, :, 0:1], c4[:, :, 3:4], ALU.add))
                    link(nc.vector.reduce_max(gsc[:, :, :].rearrange("p t g -> p (t g)"), pairs[:, :, :], X))
                    other = gsc[:, :, :].unsqueeze(2).to_broadcast([P, TT, G, G])
                    mine = gsc[:, :, :].unsqueeze(3).to_broadcast([P, TT, G, G])
                    step(tt(g_gt[:, :, :, :], other, mine, ALU.is_gt))
                    link(tt(g_ge[:, :, :, :], other, mine, ALU.is_ge))
                    link(tt(g_ge[:, :, :, :], g_ge[:, :, :, :], lower[:, :, :, :], ALU.mult))
                    link(tt(g_gt[:, :, :, :], g_gt[:, :, :, :], g_ge[:, :, :, :], ALU.max))
                    link(nc.vector.reduce_sum(g_rank[:, :], g_gt[:, :, :, :].rearrange("p t g x -> p (t g) x"), X))
                    link(nc.vector.tensor_scalar(g_in[:, :], g_rank[:, :], TOPK_G - 0.5, None, ALU.is_lt))
                    step(tt(c4, c4, g_in[:, :].unsqueeze(2).to_broadcast([P, TT * G, EG]), ALU.mult))
                    dve.drain()
                    for j in range(TT):
                        last = nc.vector.max(top8[:, j, :], cho[:, j, :])
                    link(last)
                    kth = top8[:, :, TOPK - 1:TOPK].to_broadcast([P, TT, E])
                    step(tt(e_gt[:, :, :], cho[:, :, :], kth, ALU.is_gt))
                else:
                    kth = top8[:, :, TOPK - 1:TOPK].to_broadcast([P, TT, E])
                    link(tt(e_eq[:, :, :], cho[:, :, :], kth, ALU.is_equal))
                    step(nc.vector.reduce_sum(n_gt[:, :], e_gt[:, :, :], X))
                    link(nc.vector.tensor_tensor_scan(e_pre[:, :, :].rearrange("p t e -> p (t e)"),
                                                      not_first[:, :, :].rearrange("p t e -> p (t e)"),
                                                      e_eq[:, :, :].rearrange("p t e -> p (t e)"),
                                                      0.0, ALU.mult, ALU.add))
                    link(tt(e_pre[:, :, :], e_pre[:, :, :], n_gt[:, :].unsqueeze(2).to_broadcast([P, TT, E]), ALU.add))
                    link(nc.vector.tensor_scalar(e_pre[:, :, :], e_pre[:, :, :], TOPK + 0.5, None, ALU.is_lt))
                    link(tt(e_eq[:, :, :], e_eq[:, :, :], e_pre[:, :, :], ALU.mult))
                    link(tt(e_gt[:, :, :], e_gt[:, :, :], e_eq[:, :, :], ALU.add))
                    link(tt(sig[:, :, :], sig[:, :, :], e_gt[:, :, :], ALU.mult))
                    link(nc.vector.reduce_sum(w_sum[:, :], sig[:, :, :], X))
                    link(nc.vector.tensor_scalar_add(w_sum[:, :], w_sum[:, :], 1e-20))
                    link(nc.vector.reciprocal(w_rec[:, :], w_sum[:, :]))
                    wait(dve, cwT_mm, nth(blk, 1, 0))
                    link(tt(cw[:, :, :], sig[:, :, :], w_rec[:, :].unsqueeze(2).to_broadcast([P, TT, E]), ALU.mult))
                    step(nc.vector.tensor_scalar(cw[:, :, :], cw[:, :, :], ROUTE_SCALE, None, ALU.mult))
                assert done[0] == {0: 1, 1: 17, 2: 30}[part]

            def attention(blk, h):
                par = blk[1] % 2
                if h == 1:
                    product(blk, 0)
                elif h == 2:
                    product(blk, 1)
                    product(blk, 2)
                elif h == 3:
                    product(blk, 3)
                elif h == 4:
                    product(blk, 4)
                    product(blk, 5)
                elif h == 5:
                    product(blk, 6)
                elif h == 6:
                    product(blk, 7)
                elif h == 8:
                    dve.wait_ge(score_mm, nth(blk, SLOTS, SLOTS))
                    nc.vector.reduce_max(s_max[:, :], psA[:, 0, :].rearrange("p (m n) -> p n m", m=L), X
                                         ).then_inc(smax_ready, 1)
                    dve.wait_ge(smax_ready, nth(blk, 1, 1))
                    nc.vector.tensor_tensor(s_sb[:, :, :], psA[:, 0, :].rearrange("p (m n) -> p m n", m=L),
                                            s_max[:, :].unsqueeze(1).to_broadcast([P, L, NN]), ALU.subtract
                                            ).then_inc(ssub_ready, 1)
                elif h == 9:
                    dve.wait_ge(exp_ready, nth(blk, 1, 1))
                    nc.vector.reduce_sum(s_sum[:, :], s_sb[:, :, :].rearrange("p m n -> p n m"), X).then_inc(ssum_ready, 1)
                    dve.wait_ge(ssum_ready, nth(blk, 2, 1))
                    nc.vector.reciprocal(s_rec[:, :], s_sum[:, :]).then_inc(ssum_ready, 1)
                    dve.wait_ge(ssum_ready, nth(blk, 2, 2))
                    nc.vector.tensor_tensor(s_sb[:, :, :], s_sb[:, :, :],
                                            s_rec[:, :].unsqueeze(1).to_broadcast([P, L, NN]), ALU.mult
                                            ).then_inc(probs_ready, 1)
                elif h == 10:
                    dve.wait_ge(probs_hi, nth(blk, 1, 1))
                    nc.vector.tensor_tensor(pr[1][:, :], s_sb[:, :, :].rearrange("p m n -> p (m n)"),
                                            pr[0][:, :].bitcast(f32), ALU.subtract).then_inc(probs_lo, 1)
                elif 11 <= h < 11 + SLOTS:
                    weighted_values(blk, h - 11)
                elif h in (19, 22):
                    ih = 0 if h == 19 else 1
                    dve.wait_ge(o_hi, nth(blk, 2, ih + 1))
                    nc.vector.tensor_tensor(xT1[1][:, ih, :], q_sb[:, ih, :], xT1[0][:, ih, :].bitcast(f32),
                                            ALU.subtract).then_inc(o_lo, 1)
                elif h == 24:
                    dve.wait_ge(outp_mm, nth(blk, 1, 1))
                    dve.wait_ge(xb_ready, nth(blk, 1, 1))
                    dve.wait_ge(h1_free, nth(blk, 1, 1))
                    nc.vector.tensor_tensor(h1[par][:, :, :].rearrange("p j d -> p (j d)"),
                                            psA[:, :, :].rearrange("p a t -> p (a t)"),
                                            xin[par][:, :, :].rearrange("p j d -> p (j d)"), ALU.add
                                            ).then_inc(h1_ready, 1)
                    dve.wait_ge(h1_ready, nth(blk, 1, 1))
                    norm_stats(1, blk, h1[par])
                elif h == 26:
                    normalise(1, blk, h1[par], v_sb)
                elif h == 28:
                    transposed_lo(1, blk)
                elif h in (30, 31, 32):
                    route(blk, h - 30)

            def head(blk, h):
                par = blk[1] % 2
                if h == 25:
                    dve.wait_ge(xin_in[par], turn(blk, 64) + 64)
                    norm_stats(0, blk, xin[par])
                elif h == 27:
                    normalise(0, blk, xin[par], k_sb)
                elif h == 29:
                    transposed_lo(0, blk)

            def block_dve(blk, att, nxt):
                for e in range(X_ALL):
                    if e + 1 < X_ALL:
                        weigh(blk, e + 1)
                    for h, last in ((2 * e, False), (2 * e + 1, True)):
                        if att is not None:
                            attention(att, h)
                        if nxt is not None:
                            head(nxt, h)
                        if last:
                            break
                        if e + 1 < X_ALL:
                            hidden_lo(blk, e + 1)
                        elif att is not None:
                            hidden_lo(att, 0)
                add_experts(blk)

            dve.wait_ge(small_in, 48)
            head((None, 0), 25)
            head((None, 0), 27)
            for k in range(PIECES_QKV):
                weight_lo(k)
            head((None, 0), 29)
            for k in range(PIECES_QKV, PIECES_ATT):
                weight_lo(k)
            dve.wait_ge(spread_ready, 1)
            k = PIECES_ATT
            for h in range(HALF):
                attention((None, 0), h)
                if h >= 3 and k < PIECES_ALL:
                    weight_lo(k)
                    k += 1
                head((None, 1), h)
            hidden_lo((None, 0), 0)
            with dve.Fori(0, B // 2 - 1) as i:
                block_dve((i, 0), (i, 1), (i, 2))
                block_dve((i, 1), (i, 2), (i, 3))
            block_dve((None, B - 2), (None, B - 1), None)
            block_dve((None, B - 1), None, None)

        @block.tensor
        def _(pe):
            pe.sem_inc(w2_mm, CREDIT)

            PASSES = [(0, 0), (0, 1), (1, 0)]

            def up(blk, e):
                x = xT2[blk[1] % 2]
                pe.wait_ge(relu_done, nth(blk, X_ALL, e + 1))
                for kh in range(KH):
                    for a, b in PASSES:
                        last = nc.tensor.matmul(psH[:, e % 2, :], W1[a][:, kh, e, :], x[b][:, kh, :],
                                                start=(kh == 0 and (a, b) == PASSES[0]),
                                                stop=(kh == KH - 1 and (a, b) == PASSES[-1]))
                last.then_inc(h_mm, 1)

            def down(blk, e):
                pe.wait_ge(hid_lo, nth(blk, X_ALL, e + 1 + CREDIT))
                if e == 0:
                    pe.wait_ge(y_added, nth(blk, 1, 1))
                for j in range(TT):
                    for a, b in PASSES:
                        last = nc.tensor.matmul(psY[:, j // 2, (j % 2) * D:(j % 2 + 1) * D],
                                                hid[a][:, e % 2, j * P:(j + 1) * P], W2[b][:, e, :],
                                                start=(e == 0 and (a, b) == PASSES[0] and j % 2 == 0),
                                                stop=(e == X_ALL - 1 and (a, b) == PASSES[-1] and j % 2 == 1),
                                                skip_group_check=True)
                last.then_inc(w2_mm, 1)

            def transpose_rows(w, blk):
                pe.wait_ge(xn_ready[w], nth(blk, 1, 1))
                src, ps = (k_sb, psA) if w == 0 else (v_sb, psB)
                if w == 0:
                    wait(pe, h1_ready, nth(blk, 1, 0))
                s = src[:, :, :].rearrange("p a t -> p (a t)").rearrange("p (j d) -> p j d", d=D)
                for kh in range(KH):
                    for j in range(TT):
                        last = nc.tensor.transpose(ps[:, kh, j * P:(j + 1) * P], s[:, j, kh * P:(kh + 1) * P],
                                                   ident[:, :])
                last.then_inc(xT_mm[w], 1)

            def qkv(blk, n):
                c, ih = QKV_ORDER[n]
                if n == 0:
                    pe.wait_ge(xT_lo[0], nth(blk, 1, 1))
                if n >= 2:
                    pe.wait_ge(qkv_ready, nth(blk, 6, n - 1))
                for kh in range(KH):
                    for a, b in PASSES:
                        last = nc.tensor.matmul(psB[:, n % 2, :], WQKV[a][:, kh, 2 * c + ih, :], xT1[b][:, kh, :],
                                                start=(kh == 0 and (a, b) == PASSES[0]),
                                                stop=(kh == KH - 1 and (a, b) == PASSES[-1]))
                last.then_inc(qkv_mm, 1)

            def score(blk, t):
                lp, ih = t // KH, t % KH
                pe.wait_ge(prod_ready, nth(blk, SLOTS, t + 1))
                if t == 0:
                    wait(pe, lg_ready, nth(blk, 1, 0))
                for li in range(2):
                    row = 64 * ih + 32 * li
                    last = nc.tensor.matmul(psA[row:row + 32, 0, :], head_sum[:, lp, :], ring[:, t % 4, li, :],
                                            start=(lp == 0), stop=(lp == LP - 1))
                last.then_inc(score_mm, 1)

            def spread_probs(blk, t):
                ih, lp = t // LP, t % LP
                if t == 0:
                    pe.wait_ge(probs_lo, nth(blk, 1, 1))
                    pe.wait_ge(qkv_ready, nth(blk, 6, 6))
                if t == 1:
                    wait(pe, cwT_ready, nth(blk, 1, 0))
                if t >= 2:
                    pe.wait_ge(av_ready, nth(blk, SLOTS, t - 1))
                ps = psB if t % 2 == 0 else psA
                for li in range(2):
                    c = ih * L + 2 * lp + li
                    nc.tensor.matmul(ps[:, li, :], spread[:, c, :], pr[0][:, :], start=True, stop=False)
                    last = nc.tensor.matmul(ps[:, li, :], spread[:, c, :], pr[1][:, :], start=False, stop=True)
                last.then_inc(spread_mm, 1)

            def out_projection(blk):
                pe.wait_ge(o_lo, nth(blk, 2, 2))
                pe.wait_ge(av_ready, nth(blk, SLOTS, SLOTS))
                for j in range(TT):
                    for ih in range(KH):
                        for a, b in PASSES:
                            last = nc.tensor.matmul(psA[:, j // 2, (j % 2) * D:(j % 2 + 1) * D],
                                                    xT1[a][:, ih, j * P:(j + 1) * P], WO[b][:, ih, :],
                                                    start=(ih == 0 and (a, b) == PASSES[0]),
                                                    stop=(ih == KH - 1 and (a, b) == PASSES[-1]))
                last.then_inc(outp_mm, 1)

            def logits(blk, nxt):
                pe.wait_ge(xT_lo[1], nth(blk, 1, 1))
                if nxt is not None:
                    pe.wait_ge(xT_lo[0], nth(nxt, 1, 1))
                x = xT2[blk[1] % 2]
                for j in range(TT):
                    for kh in range(KH):
                        for a in range(2):
                            last = nc.tensor.matmul(psA[:, 0, j * 2 * E:(j + 1) * 2 * E],
                                                    x[a][:, kh, j * P:(j + 1) * P],
                                                    WG[:, kh, :, :].rearrange("p a e -> p (a e)"),
                                                    start=(kh == 0 and a == 0), stop=(kh == KH - 1 and a == 1))
                last.then_inc(logit_mm, 1)

            def weights_transpose(blk):
                pe.wait_ge(route_step, nth(blk, ROUTE_STEPS, ROUTE_STEPS))
                for j in range(TT):
                    last = nc.tensor.transpose(psA[0:E, 1, j * P:(j + 1) * P], cw[:, j, :], ident[:, :])
                last.then_inc(cwT_mm, 1)

            def attention(blk, h, nxt):
                if h == 0:
                    qkv(blk, 0)
                    qkv(blk, 1)
                elif h == 1:
                    qkv(blk, 2)
                    qkv(blk, 3)
                elif h in (2, 3):
                    qkv(blk, h + 2)
                    if h == 3:
                        score(blk, 0)
                        score(blk, 1)
                elif h == 4:
                    score(blk, 2)
                    score(blk, 3)
                elif h == 5:
                    score(blk, 4)
                    score(blk, 5)
                elif h in (6, 7):
                    score(blk, h)
                elif h == 11:
                    spread_probs(blk, 0)
                    spread_probs(blk, 1)
                elif 12 <= h < 12 + SLOTS - 2:
                    spread_probs(blk, h - 10)
                elif h == 23:
                    out_projection(blk)
                elif h == 27:
                    transpose_rows(1, blk)
                elif h == 30:
                    logits(blk, nxt)

            def head(blk, h):
                if h == 28:
                    transpose_rows(0, blk)

            def block_pe(blk, att, nxt):
                for e in range(X_ALL):
                    if e + 2 < X_ALL:
                        up(blk, e + 2)
                    elif att is not None:
                        up(att, e + 2 - X_ALL)
                    for h, last in ((2 * e, False), (2 * e + 1, True)):
                        if att is not None:
                            attention(att, h, nxt)
                        if nxt is not None:
                            head(nxt, h)
                        if last:
                            break
                        down(blk, e)
                        if e == 0:
                            weights_transpose(blk)

            pe.wait_ge(const_step, CONST_IDENT)
            head((None, 0), 28)
            pe.wait_ge(w_lo, PIECES_ATT)
            pe.wait_ge(const_step, CONST_ALL)
            pe.wait_ge(spread_ready, 1)
            for h in range(HALF):
                attention((None, 0), h, (None, 1))
                head((None, 1), h)
            pe.wait_ge(w_lo, PIECES_ALL)
            up((None, 0), 0)
            up((None, 0), 1)
            with pe.Fori(0, B // 2 - 1) as i:
                block_pe((i, 0), (i, 1), (i, 2))
                block_pe((i, 1), (i, 2), (i, 3))
            block_pe((None, B - 2), (None, B - 1), None)
            block_pe((None, B - 1), None, None)


def kernel(x, L0_tok_weight, L0_attn_qkv_proj, L0_attn_qkv_bias, L0_attn_out_proj, L0_attn_out_bias,
           L0_ffn_Wg, L0_ffn_bias_corr, L0_ffn_W1, L0_ffn_W2, L0_ffn_Ws1, L0_ffn_Ws2):
    import numpy as np
    import concourse.bacc as bacc
    from concourse.bass_utils import run_bass_kernel_spmd

    c = np.ascontiguousarray
    L, N = x.shape
    D = L0_tok_weight.shape[1]
    P, KH = 128, D // 128
    E, I, _ = L0_ffn_W1.shape
    SH = L0_ffn_Ws1.shape[0] // P
    x = np.asarray(x)
    arrays = {
        "ids": c(x.reshape(L // 2, 2, N // 64, 64).transpose(1, 3, 2, 0).reshape(P, -1)),
        "table": c(L0_tok_weight),
        "wqkv_t": c(np.asarray(L0_attn_qkv_proj).reshape(D, 3, KH, P).transpose(3, 2, 1, 0).reshape(P, -1)),
        "bqkv": c(np.asarray(L0_attn_qkv_bias).reshape(KH, P, 3).transpose(1, 2, 0).reshape(P, -1)),
        "wo_t": c(np.asarray(L0_attn_out_proj).reshape(D, KH, P).transpose(2, 1, 0).reshape(P, -1)),
        "bo": c(np.asarray(L0_attn_out_bias).reshape(1, D)),
        "wg_t": c(np.asarray(L0_ffn_Wg).reshape(E, KH, P).transpose(2, 1, 0).reshape(P, -1)),
        "bias_corr": c(np.asarray(L0_ffn_bias_corr).reshape(1, E)),
        "w1_t": c(np.asarray(L0_ffn_W1).reshape(E, I, KH, P).transpose(3, 2, 0, 1).reshape(P, -1)),
        "ws1_t": c(np.asarray(L0_ffn_Ws1).reshape(SH, P, KH, P).transpose(3, 2, 0, 1).reshape(P, -1)),
        "w2_t": c(np.asarray(L0_ffn_W2).transpose(2, 0, 1).reshape(P, -1)),
        "ws2_t": c(np.asarray(L0_ffn_Ws2).reshape(D, SH, P).transpose(2, 1, 0).reshape(P, -1)),
    }
    nc = bacc.Bacc("TRN2", target_bir_lowering=False, num_devices=1)
    args = [nc.dram_tensor(k, a.shape, mybir.dt.from_np(a.dtype), kind="ExternalInput").ap() for k, a in arrays.items()]
    out = nc.dram_tensor("out_0", (L, N, D), mybir.dt.float32, kind="ExternalOutput").ap()
    lm_tower_layer(nc, *args, out)
    r = run_bass_kernel_spmd(nc, [arrays], core_ids=[0])
    return r.results[0]["out_0"]
```

```python
import concourse.bass as bass
from concourse import mybir
from contextlib import ExitStack


def lm_tower_layer(nc: bass.Bass, ids, table, wqkv_t, bqkv, wo_t, bo, wg_t, bias_corr,
                   w1_t, ws1_t, w2_t, ws2_t, out):
    f32 = mybir.dt.float32
    f32r = mybir.dt.float32r
    i32 = mybir.dt.int32
    ALU = mybir.AluOpType
    ACT = mybir.ActivationFunctionType
    X = mybir.AxisListType.X

    P = 128
    VOCAB, D = table.shape
    L, N = out.shape[0], out.shape[1]
    NH = 16
    DH = D // NH
    HH = P // DH
    KH = D // P
    NN = 64
    T = NN * L
    TT = T // P
    B = N // NN
    E = wg_t.shape[1] // KH
    SH = ws1_t.shape[1] // (KH * P)
    X_ALL = E + SH
    G = 4
    EG = E // G
    TOPK_G, TOPK, ROUTE_SCALE = 2, 4, 2.5
    EPS = 1e-5
    ATT_SCALE = float(DH) ** -0.5
    LP = L // 2
    SLOTS = KH * LP
    QN = 2
    QS = E // QN
    HALF = 2 * X_ALL

    def nth(blk, per, k):
        i, off = blk
        return off * per + k if i is None else i * (2 * per) + (off * per + k)

    def turn(blk, per):
        i, off = blk
        return (off // 2) * per if i is None else i * per + (off // 2) * per

    def after(blk, d):
        return (blk[0], blk[1] + d)

    def block_ds(blk):
        return bass.ds(nth(blk, 1, 0), 1)

    def wait(eng, sem, value):
        if not isinstance(value, int) or value > 0:
            eng.wait_ge(sem, value)

    def wait_apart(eng, sem, value):
        value = value if isinstance(value, int) else eng.snap(value)
        eng.wait_ge(sem, 1)
        wait(eng, sem, value)

    ctx = ExitStack()
    with ctx:
        def sb(name, shape, dt=f32):
            return ctx.enter_context(nc.sbuf_tensor(name, shape, dt))

        def pb(name, shape):
            return ctx.enter_context(nc.psum_tensor(name, shape, f32))

        def sem(name):
            return ctx.enter_context(nc.semaphore(name))

        W1 = [sb(f"w1_{p}", [P, KH, X_ALL, P], f32r) for p in ("hi", "lo")]
        W2 = [sb(f"w2_{p}", [P, X_ALL, D], f32r) for p in ("hi", "lo")]
        WQKV = [sb(f"wqkv_{p}", [P, KH, 6, P], f32r) for p in ("hi", "lo")]
        WO = [sb(f"wo_{p}", [P, KH, D], f32r) for p in ("hi", "lo")]
        WG = sb("wg_hi_lo", [P, KH, 2, E], f32r)
        ident = sb("ident", [P, P])
        head_sum = sb("head_sum", [P, 4, 32])
        spread = sb("spread", [P, L, P], f32r)
        bq = sb("bqkv_sb", [P, 6])
        bo_sb = sb("bo_sb", [P, D])
        bc_sb = sb("bias_corr_sb", [P, E])
        half_neg = sb("half_neg", [P, TT])
        lower = sb("lower", [P, TT, G, G])
        not_first = sb("not_first", [P, TT, E])
        idx = sb("idx", [P, B * TT], i32)
        idx_now = sb("idx_now", [P, TT], i32)
        xin = [sb(f"xin{p}", [P, TT, D]) for p in range(2)]
        h1 = [sb(f"h1_{p}", [P, TT, D]) for p in range(2)]
        xT1 = [sb(f"xT1_{p}", [P, KH, T], f32r) for p in ("hi", "lo")]
        xT2 = [[sb(f"xT2_{p}{q}", [P, KH, T], f32r) for p in ("hi", "lo")] for q in range(2)]
        q_sb = sb("q_sb", [P, KH, T])
        k_sb = sb("k_sb", [P, KH, T])
        v_sb = sb("v_sb", [P, KH, T])
        ring = sb("ring", [P, 4, 2, T])
        s_sb = sb("s_sb", [P, L, NN])
        pr = [sb(f"probs{ih}", [P, T], f32r) for ih in range(KH)]
        s_max = sb("s_max", [P, NN])
        s_sum = sb("s_sum", [P, NN])
        s_rec = sb("s_rec", [P, NN])
        stats = [sb(f"stats{w}", [P, TT, 6]) for w in range(2)]
        mv = [sb(f"mv{w}", [P, 3, TT]) for w in range(2)]
        veps = [sb(f"veps{w}", [P, TT]) for w in range(2)]
        rstd = [sb(f"rstd{w}", [P, TT]) for w in range(2)]
        lg = sb("lg", [P, TT, 2, E])
        lgt = sb("lgt", [P, TT, E])
        sig = sb("sig", [P, TT, E])
        cho = sb("cho", [P, TT, E])
        pairs = sb("pairs", [P, TT * G, 6])
        gsc = sb("gsc", [P, TT, G])
        g_gt = sb("g_gt", [P, TT, G, G])
        g_ge = sb("g_ge", [P, TT, G, G])
        g_rank = sb("g_rank", [P, TT * G])
        g_in = sb("g_in", [P, TT * G])
        top8 = sb("top8", [P, TT, 8])
        e_gt = sb("e_gt", [P, TT, E])
        e_eq = sb("e_eq", [P, TT, E])
        e_pre = sb("e_pre", [P, TT, E])
        n_gt = sb("n_gt", [P, TT])
        w_sum = sb("w_sum", [P, TT])
        w_rec = sb("w_rec", [P, TT])
        cw = sb("cw", [P, TT, E])
        cwT = sb("cwT", [E, T])
        cwB = sb("cwB", [P, 2, QN, T])
        stage = cwB[:, :, :, :].rearrange("p a b t -> p a (b t)")
        r_sb = sb("r_sb", [P, 2, T])
        p_sb = sb("p_sb", [P, 2, T])
        hid = [sb(f"hid_{p}", [P, 2, T], f32r) for p in ("hi", "lo")]

        psH = pb("psH", [P, 2, T])
        psY = pb("psY", [P, 2, T])
        psA = pb("psA", [P, 2, T])
        psB = pb("psB", [P, 2, T])

        cw_dram = nc.dram_tensor("cw_dram", (B, E * T), f32, kind="Internal").ap()

        idx_in = sem("idx_in")
        small_in = sem("small_in")
        w_in = [sem("w_in0"), sem("w_in1")]
        w_hi = sem("w_hi")
        w_lo = sem("w_lo")
        const_step = sem("const_step")
        spread_ready = sem("spread_ready")
        idx_now_ready = sem("idx_now_ready")
        xin_in = [sem("xin_in0"), sem("xin_in1")]
        ln_stats = [sem("ln1_stats"), sem("ln2_stats")]
        ln_aggr = [sem("ln1_aggr"), sem("ln2_aggr")]
        ln_rstd = [sem("ln1_rstd"), sem("ln2_rstd")]
        xn_ready = [sem("xn1_ready"), sem("xn2_ready")]
        xT_mm = [sem("xT1_mm"), sem("xT2_mm")]
        xT_hi = [sem("xT1_hi_ready"), sem("xT2_hi_ready")]
        xT_lo = [sem("xT1_lo_ready"), sem("xT2_lo_ready")]
        xb_ready = sem("xb_ready")
        qkv_mm = sem("qkv_mm")
        qkv_ready = sem("qkv_ready")
        prod_ready = sem("prod_ready")
        score_mm = sem("score_mm")
        smax_ready = sem("smax_ready")
        ssub_ready = sem("ssub_ready")
        exp_ready = sem("exp_ready")
        ssum_ready = sem("ssum_ready")
        probs_ready = sem("probs_ready")
        probs_hi = sem("probs_hi_ready")
        probs_lo = sem("probs_lo_ready")
        spread_mm = sem("spread_mm")
        av_ready = sem("av_ready")
        msum1 = sem("msum1")
        msum2 = sem("msum2")
        o_ready = sem("o_ready")
        o_hi = sem("o_hi_ready")
        o_lo = sem("o_lo_ready")
        outp_mm = sem("outp_mm")
        h1_ready = sem("h1_ready")
        logit_mm = sem("logit_mm")
        lg_ready = sem("lg_ready")
        route_step = sem("route_step")
        sigexp_ready = sem("sigexp_ready")
        cwT_mm = sem("cwT_mm")
        cwT_ready = sem("cwT_ready")
        cwT_stored = sem("cwT_stored")
        cwB_in = [sem("cwB_in0"), sem("cwB_in1")]
        h_mm = sem("h_mm")
        relu_done = sem("relu_done")
        sq_done = sem("sq_done")
        p_ready = sem("p_ready")
        hid_hi = sem("hid_hi_ready")
        hid_lo = sem("hid_lo_ready")
        w2_mm = sem("w2_mm")
        y_added = sem("y_added")
        out_stored = sem("out_stored")
        h1_free = sem("h1_free")
        CREDIT = 2
        ROUTE_FIRST = [0, 1, 8, 14, 17, 23, 30]
        ROUTE_STEPS = ROUTE_FIRST[-1]
        CONST_IDENT = 3
        CONST_ALL = 15

        def flat(t):
            return t[:, :, :, :].rearrange("p a b c -> p (a b c)") if len(t.shape) == 4 else \
                t[:, :, :].rearrange("p a b -> p (a b)")

        PIECES = []

        def cut(src, dst, base, total, step):
            for at in range(0, total, step):
                n = min(step, total - at)
                PIECES.append((src[:, at:at + n], n, [flat(d)[:, base + at:base + at + n] for d in dst]))

        cut(wqkv_t, WQKV, 0, KH * 6 * P, 768)
        PIECES_QKV = len(PIECES)
        cut(wo_t, WO, 0, KH * D, KH * D)
        for kh in range(KH):
            PIECES.append((wg_t[:, kh * E:(kh + 1) * E], E, [WG[:, kh, s, :] for s in range(2)]))
        PIECES_ATT = len(PIECES)
        for kh in range(KH):
            for src, first, n_e in ((ws1_t, 0, SH), (w1_t, SH, E)):
                cut(src[:, kh * n_e * P:(kh + 1) * n_e * P], W1, (kh * X_ALL + first) * P, n_e * P, 1024)
        cut(ws2_t, W2, 0, SH * D, 1024)
        cut(w2_t, W2, SH * D, E * D, 1024)
        PIECES_ALL = len(PIECES)

        SCORES = {0: (0, 1), 2: (2, 3), 4: (4, 5), 6: (6, 7)}
        SPREADS = {10: (0, 1), **{9 + t: (t,) for t in range(2, SLOTS)}}
        OUT_PROJECTION, T2, LOGITS, WEIGHTS = 23, 28, 30, 35
        A_EXP, A_PROBS, A_OUT, A_T2, A_LOGITS, A_WEIGHTS = 7, 8, (16, 20), 28, 31, 35
        V_PRODUCTS = [34, 35, 0, 1, 2, 3, 4, 5]
        V_MAX, V_SUM, V_PROBS, V_VALUES, V_OUT = 6, 7, 8, 10, (18, 21)
        V_H1, V_NORM2, V_T2 = 24, 26, 29
        V_ROUTE = [31, 31, 32, 33, 33, 34]
        V_STATS1, V_NORM1, V_T1, T1, A_T1 = 6, 8, 25, 22, 24
        QKV_AT = [27, 28, 29, 30, 31, 32]

        QKV_ORDER = [(0, 0), (1, 0), (0, 1), (1, 1), (2, 0), (2, 1)]
        QKV_SB = [q_sb, k_sb, v_sb]

        block = ctx.enter_context(nc.Block())

        @block.sync
        def _(sp):
            sp.sem_inc(h1_free, 2)
            sp.dma_start(idx[:, :], ids).then_inc(idx_in, 16)
            sp.dma_start(bq[:, :], bqkv).then_inc(small_in, 16)
            sp.dma_start(bo_sb[:, :], bo.partition_broadcast(P)).then_inc(small_in, 16)
            sp.dma_start(bc_sb[:, :], bias_corr.partition_broadcast(P)).then_inc(small_in, 16)
            for k, (src, n, _dst) in enumerate(PIECES):
                if k >= 2:
                    sp.wait_ge(w_lo, k - 1)
                sp.dma_start(stage[:, k % 2, 0:n], src).then_inc(w_in[k % 2], 16)
            sp.wait_ge(w_lo, PIECES_ALL)

            out_v = out.rearrange("(j q) (b n) d -> q b n j d", q=2, n=NN)

            def weights_in(blk, g):
                src = cw_dram[block_ds(blk), g * QN * T:(g + 1) * QN * T]
                sp.dma_start(cwB[:, g % 2, :, :].rearrange("p a t -> p (a t)"),
                             src.partition_broadcast(P)).then_inc(cwB_in[g % 2], 16)

            def weights_io(blk):
                sp.wait_ge(cwT_ready, nth(blk, 1, 1))
                sp.dma_start(cw_dram[block_ds(blk), :].rearrange("o (e t) -> (o e) t", t=T),
                             cwT[:, :]).then_inc(cwT_stored, 16)
                sp.wait_ge(cwT_stored, nth(blk, 16, 16))
                weights_in(blk, 0)
                weights_in(blk, 1)

            def block_io(blk, att):
                for g in range(2, QS):
                    sp.wait_ge(p_ready, nth(blk, E, QN * (g - 1)))
                    weights_in(blk, g)
                if att is not None:
                    weights_io(att)
                sp.wait_ge(y_added, nth(blk, 1, 2))
                par = blk[1] % 2
                for q in range(2):
                    sp.dma_start(out_v[q, block_ds(blk), :, :, :].rearrange("o n j d -> (o n) j d"),
                                 h1[par][q * NN:(q + 1) * NN, :, :]).then_inc(out_stored, 16)
                sp.wait_ge(out_stored, nth(blk, 32, 32))
                sp.sem_inc(h1_free, 1)

            weights_io((None, 0))
            with sp.Fori(0, B // 2 - 1) as i:
                block_io((i, 0), (i, 1))
                block_io((i, 1), (i, 2))
            block_io((None, B - 2), (None, B - 1))
            block_io((None, B - 1), None)

        @block.gpsimd
        def _(pool):
            steps = [0]

            def link(ins):
                steps[0] += 1
                ins.then_inc(const_step, 1)
                pool.wait_ge(const_step, steps[0])

            def gather(blk):
                wait(pool, h1_ready, nth(blk, 1, -1))
                nc.gpsimd.tensor_copy(idx_now[:, :], idx[:, bass.ds(nth(blk, TT, 0), TT)]).then_inc(idx_now_ready, 1)
                wait_apart(pool, idx_now_ready, nth(blk, 1, 1) - 2)
                par = blk[1] % 2
                for j in range(TT):
                    nc.gpsimd.indirect_dma_start(xin[par][:, j, :], None, table,
                                                 bass.IndirectOffsetOnAxis(idx_now[:, j:j + 1], 0)
                                                 ).then_inc(xin_in[par], 16)

            def gather_first(b):
                for j in range(TT):
                    nc.gpsimd.indirect_dma_start(xin[b][:, j, :], None, table,
                                                 bass.IndirectOffsetOnAxis(idx[:, b * TT + j:b * TT + j + 1], 0)
                                                 ).then_inc(xin_in[b], 16)

            def rstd_of(w, blk):
                pool.wait_ge(ln_aggr[w], nth(blk, 1, 1))
                nc.gpsimd.tensor_tensor(rstd[w][:, :], veps[w][:, :], half_neg[:, :], ALU.pow).then_inc(ln_rstd[w], 1)

            def position_sum(blk, t):
                a = ring[:, t % 4, :, :].rearrange("p l (m n) -> p l m n", m=L)
                ih, lp = t // LP, t % LP
                pool.wait_ge(av_ready, nth(blk, SLOTS, t + 1))
                nc.gpsimd.tensor_tensor(a[:, :, 0:4, :], a[:, :, 0:4, :], a[:, :, 4:8, :], ALU.add).then_inc(msum1, 1)
                pool.wait_ge(msum1, nth(blk, SLOTS, t + 1))
                nc.gpsimd.tensor_tensor(a[:, :, 0:2, :], a[:, :, 0:2, :], a[:, :, 2:4, :], ALU.add).then_inc(msum2, 1)
                pool.wait_ge(msum2, nth(blk, SLOTS, t + 1))
                o = q_sb[:, ih, 2 * lp * NN:(2 * lp + 2) * NN].rearrange("p (l n) -> p l n", l=2)
                nc.gpsimd.tensor_tensor(o, a[:, :, 0, :], a[:, :, 1, :], ALU.add).then_inc(o_ready, 1)

            def head(blk):
                rstd_of(0, blk)
                pool.wait_ge(xn_ready[0], nth(blk, 1, 1))
                par = blk[1] % 2
                nc.gpsimd.tensor_tensor(xin[par][:, :, :], xin[par][:, :, :],
                                        bo_sb[:, :].unsqueeze(1).to_broadcast([P, TT, D]), ALU.add).then_inc(xb_ready, 1)

            def main(blk):
                for t in range(SLOTS):
                    position_sum(blk, t)
                rstd_of(1, blk)

            pool.wait_ge(idx_in, 16)
            gather_first(0)
            link(nc.gpsimd.memset(half_neg[:, :], -0.5))
            link(nc.gpsimd.memset(ident[:, :], 0.0))
            link(nc.gpsimd.affine_select(out=ident[:, :], in_=ident[:, :], compare_op=ALU.not_equal, fill=1.0,
                                         base=0, pattern=[[-1, P]], channel_multiplier=1))
            gather_first(1)
            pool.wait_ge(small_in, 48)
            head((None, 0))
            link(nc.gpsimd.memset(head_sum[:, :, :], 1.0))
            link(nc.gpsimd.affine_select(out=head_sum[:, :, :], in_=head_sum[:, :, :], compare_op=ALU.is_ge, fill=0.0,
                                         base=0, pattern=[[P, 4], [-DH, 32]], channel_multiplier=1))
            link(nc.gpsimd.affine_select(out=head_sum[:, :, :], in_=head_sum[:, :, :], compare_op=ALU.is_ge, fill=0.0,
                                         base=DH - 1, pattern=[[-P, 4], [DH, 32]], channel_multiplier=-1))
            sp_f = ring[:, 0, :, :].rearrange("p b c -> p (b c)")
            link(nc.gpsimd.memset(sp_f, 0.0))
            v = sp_f.rearrange("p (a b h d) -> p a b h d", a=LP, b=2, h=HH)
            for ih in range(KH):
                for b in range(2):
                    link(nc.gpsimd.affine_select(out=v[:, :, b, :, :], in_=v[:, :, b, :, :], compare_op=ALU.not_equal,
                                                 fill=1.0, base=-(64 * ih + 32 * b), channel_multiplier=1,
                                                 pattern=[[-HH, LP], [-1, HH], [0, DH]]))
            link(nc.gpsimd.memset(lower[:, :, :, :], 1.0))
            link(nc.gpsimd.affine_select(out=lower[:, :, :, :], in_=lower[:, :, :, :], compare_op=ALU.is_gt, fill=0.0,
                                         base=0, pattern=[[0, TT], [1, G], [-1, G]], channel_multiplier=0))
            link(nc.gpsimd.memset(not_first[:, :, :], 1.0))
            link(nc.gpsimd.affine_select(out=not_first[:, :, :], in_=not_first[:, :, :], compare_op=ALU.is_gt,
                                         fill=0.0, base=0, pattern=[[0, TT], [1, E]], channel_multiplier=0))
            assert steps[0] == CONST_ALL
            head((None, 1))
            main((None, 0))

            def block_pool(blk):
                gather(after(blk, 2))
                head(after(blk, 2))
                main(after(blk, 1))

            with pool.Fori(0, B // 2 - 1) as i:
                block_pool((i, 0))
                block_pool((i, 1))
            main((None, B - 1))

        @block.scalar
        def _(act):
            act.sem_inc(relu_done, CREDIT)
            act.sem_inc(hid_hi, CREDIT)

            def weight_hi(k):
                src, n, dst = PIECES[k]
                act.wait_ge(w_in[k % 2], 16 * (k // 2 + 1))
                nc.scalar.copy(dst[0], stage[:, k % 2, 0:n]).then_inc(w_hi, 1)

            def relu_square(blk, e):
                act.wait_ge(h_mm, nth(blk, X_ALL, e + 1))
                act.wait_ge(hid_lo, nth(blk, X_ALL, e + 1))
                nc.scalar.activation(r_sb[:, e % 2, :], psH[:, e % 2, :], ACT.Relu).then_inc(relu_done, 1)
                act.wait_ge(relu_done, nth(blk, X_ALL, e + 1 + CREDIT))
                nc.scalar.activation(r_sb[:, e % 2, :], r_sb[:, e % 2, :], ACT.Square).then_inc(sq_done, 1)

            def hidden_hi(blk, e):
                if e < SH:
                    act.wait_ge(sq_done, nth(blk, X_ALL, e + 1))
                    src = r_sb
                else:
                    act.wait_ge(p_ready, nth(blk, E, e - SH + 1))
                    src = p_sb
                act.wait_ge(w2_mm, nth(blk, X_ALL, e + 1))
                nc.scalar.copy(hid[0][:, e % 2, :], src[:, e % 2, :]).then_inc(hid_hi, 1)

            def transposed_hi(w, blk):
                act.wait_ge(xT_mm[w], nth(blk, 1, 1))
                if w == 0:
                    wait(act, outp_mm, nth(blk, 1, 0))
                    dst, src = xT1[0], psB
                else:
                    dst, src = xT2[blk[1] % 2][0], psA
                nc.scalar.copy(dst[:, :, :], src[:, :, :]).then_inc(xT_hi[w], 1)

            def qkv_out(blk, n):
                c, ih = QKV_ORDER[n]
                act.wait_ge(qkv_mm, nth(blk, 6, n + 1))
                if n == 0:
                    wait(act, o_lo, nth(blk, 2, 0))
                if n == 4:
                    wait(act, xT_mm[1], nth(blk, 1, 0))
                nc.scalar.activation(QKV_SB[c][:, ih, :], psB[:, n % 2, :], ACT.Identity,
                                     bias=bq[:, 2 * c + ih:2 * c + ih + 1]).then_inc(qkv_ready, 1)

            def weights_out(blk):
                act.wait_ge(cwT_mm, nth(blk, 1, 1))
                nc.scalar.copy(cwT[:, :], psA[0:E, 1, :]).then_inc(cwT_ready, 1)

            def attention(blk, h):
                if h == A_EXP:
                    act.wait_ge(ssub_ready, nth(blk, 1, 1))
                    nc.scalar.activation(s_sb[:, :, :], s_sb[:, :, :], ACT.Exp, scale=ATT_SCALE).then_inc(exp_ready, 1)
                if h == A_PROBS:
                    act.wait_ge(probs_ready, nth(blk, 1, 1))
                    wait(act, spread_mm, nth(blk, SLOTS, 0))
                    for ih in range(KH):
                        rows = slice(64 * ih, 64 * ih + 64)
                        last = nc.scalar.copy(pr[ih][rows, :], s_sb[rows, :, :].rearrange("p m n -> p (m n)"))
                    last.then_inc(probs_hi, 1)
                if h in A_OUT:
                    ih = A_OUT.index(h)
                    act.wait_ge(o_ready, nth(blk, SLOTS, LP * (ih + 1)))
                    act.wait_ge(qkv_mm, nth(blk, 6, 6))
                    nc.scalar.copy(xT1[0][:, ih, :], q_sb[:, ih, :]).then_inc(o_hi, 1)
                if h == A_T2:
                    transposed_hi(1, blk)
                if h == A_LOGITS:
                    act.wait_ge(logit_mm, nth(blk, 1, 1))
                    wait(act, route_step, nth(blk, ROUTE_STEPS, 1 - ROUTE_STEPS))
                    nc.scalar.copy(lg[:, :, :, :].rearrange("p a b c -> p (a b c)"),
                                   psA[:, 0, 0:TT * 2 * E]).then_inc(lg_ready, 1)
                    act.wait_ge(route_step, nth(blk, ROUTE_STEPS, 1))
                    nc.scalar.activation(sig[:, :, :], lgt[:, :, :], ACT.Exp, scale=-1.0).then_inc(sigexp_ready, 1)
                if h == A_WEIGHTS:
                    weights_out(blk)

            def head(blk, h):
                if h == A_T1:
                    transposed_hi(0, blk)
                if h in QKV_AT:
                    qkv_out(blk, QKV_AT.index(h))

            def block_act(blk, att, nxt):
                for e in range(X_ALL):
                    if e + 1 < X_ALL:
                        relu_square(blk, e + 1)
                    elif att is not None:
                        relu_square(att, 0)
                    for h, last in ((2 * e, False), (2 * e + 1, True)):
                        if att is not None:
                            attention(att, h)
                        if nxt is not None:
                            head(nxt, h)
                        if last:
                            break
                        if e + 1 < X_ALL:
                            hidden_hi(blk, e + 1)
                        elif att is not None:
                            hidden_hi(att, 0)

            act.wait_ge(small_in, 48)
            for k in range(PIECES_QKV):
                weight_hi(k)
            act.wait_ge(const_step, CONST_IDENT)
            for h in range(HALF):
                head((None, 0), h)
            for k in range(PIECES_QKV, PIECES_ATT):
                weight_hi(k)
            act.wait_ge(const_step, CONST_ALL)
            nc.scalar.copy(spread[:, :, :].rearrange("p a b -> p (a b)"),
                           ring[:, 0, :, :].rearrange("p b c -> p (b c)")).then_inc(spread_ready, 1)
            k = PIECES_ATT
            for h in range(HALF):
                attention((None, 0), h)
                if k < PIECES_ALL:
                    weight_hi(k)
                    k += 1
                head((None, 1), h)
            assert k == PIECES_ALL
            relu_square((None, 0), 0)
            hidden_hi((None, 0), 0)
            with act.Fori(0, B // 2 - 1) as i:
                block_act((i, 0), (i, 1), (i, 2))
                block_act((i, 1), (i, 2), (i, 3))
            block_act((None, B - 2), (None, B - 1), None)
            block_act((None, B - 1), None, None)

        @block.vector
        def _(dve):
            dve.sem_inc(hid_lo, CREDIT)
            dve.sem_inc(y_added, 1)

            def weight_lo(k):
                src, n, dst = PIECES[k]
                dve.wait_ge(w_hi, k + 1)
                nc.vector.tensor_tensor(dst[1], stage[:, k % 2, 0:n], dst[0].bitcast(f32), ALU.subtract).then_inc(w_lo, 1)

            def weigh(blk, e):
                if e < SH:
                    return
                r = e - SH
                dve.wait_ge(sq_done, nth(blk, X_ALL, e + 1))
                if r % QN == 0:
                    g = r // QN
                    dve.wait_ge(cwB_in[g % 2], nth(blk, 16 * QS // 2, 16 * (g // 2 + 1)))
                dve.wait_ge(hid_hi, nth(blk, X_ALL, e + 1))
                nc.vector.tensor_tensor(p_sb[:, e % 2, :], r_sb[:, e % 2, :],
                                        cwB[:, (r // QN) % 2, r % QN, :], ALU.mult).then_inc(p_ready, 1)

            def hidden_lo(blk, e):
                src = r_sb if e < SH else p_sb
                dve.wait_ge(hid_hi, nth(blk, X_ALL, e + 1 + CREDIT))
                nc.vector.tensor_tensor(hid[1][:, e % 2, :], src[:, e % 2, :],
                                        hid[0][:, e % 2, :].bitcast(f32), ALU.subtract).then_inc(hid_lo, 1)

            def add_experts(blk):
                par = blk[1] % 2
                dve.wait_ge(w2_mm, nth(blk, X_ALL, X_ALL + CREDIT))
                nc.vector.tensor_tensor(h1[par][:, :, :].rearrange("p j d -> p (j d)"),
                                        psY[:, :, :].rearrange("p a t -> p (a t)"),
                                        h1[par][:, :, :].rearrange("p j d -> p (j d)"), ALU.add).then_inc(y_added, 1)

            def norm_stats(w, blk, src):
                for j in range(TT):
                    last = nc.vector.bn_stats(stats[w][:, j, :], src[:, j, :])
                last.then_inc(ln_stats[w], 1)
                dve.wait_ge(ln_stats[w], nth(blk, 3, 1))
                st, m = stats[w], mv[w]
                nc.vector.tensor_tensor(m[:, 0, :], st[:, :, 1], st[:, :, 4], ALU.add)
                nc.vector.tensor_tensor(m[:, 1, :], st[:, :, 1], st[:, :, 4], ALU.subtract)
                nc.vector.tensor_tensor(m[:, 2, :], st[:, :, 2], st[:, :, 5], ALU.add).then_inc(ln_stats[w], 1)
                dve.wait_ge(ln_stats[w], nth(blk, 3, 2))
                nc.vector.tensor_tensor(m[:, 1, :], m[:, 1, :], m[:, 1, :], ALU.mult)
                nc.vector.tensor_scalar(m[:, 0, :], m[:, 0, :], 0.5, None, ALU.mult)
                nc.vector.tensor_scalar(m[:, 2, :], m[:, 2, :], 1.0 / D, EPS, ALU.mult, ALU.add).then_inc(ln_stats[w], 1)
                dve.wait_ge(ln_stats[w], nth(blk, 3, 3))
                nc.vector.scalar_tensor_tensor(veps[w][:, :], m[:, 1, :], 0.25, m[:, 2, :], ALU.mult, ALU.add
                                               ).then_inc(ln_aggr[w], 1)

            def normalise(w, blk, src, dst):
                dve.wait_ge(ln_rstd[w], nth(blk, 1, 1))
                d = dst[:, :, :].rearrange("p a t -> p (a t)").rearrange("p (j d) -> p j d", d=D)
                for j in range(TT):
                    last = nc.vector.tensor_scalar(d[:, j, :], src[:, j, :], mv[w][:, 0, j:j + 1], rstd[w][:, j:j + 1],
                                                   ALU.subtract, ALU.mult)
                last.then_inc(xn_ready[w], 1)

            def transposed_lo(w, blk):
                src, dst = (psB, xT1) if w == 0 else (psA, xT2[blk[1] % 2])
                dve.wait_ge(xT_hi[w], nth(blk, 1, 1))
                nc.vector.tensor_tensor(dst[1][:, :, :], src[:, :, :], dst[0][:, :, :].bitcast(f32),
                                        ALU.subtract).then_inc(xT_lo[w], 1)

            def product(blk, t):
                lp, ih = t // KH, t % KH
                if t == 0:
                    dve.wait_ge(qkv_ready, nth(blk, 6, 2))
                elif t == 1:
                    dve.wait_ge(qkv_ready, nth(blk, 6, 4))
                if t < 4:
                    wait(dve, o_ready, nth(blk, SLOTS, t + 5 - SLOTS))
                else:
                    dve.wait_ge(score_mm, nth(blk, SLOTS, t - 3))
                qv = q_sb[:, ih, 2 * lp * NN:(2 * lp + 2) * NN].rearrange("p (l n) -> p l n", l=2)
                kv = k_sb[:, ih, :].rearrange("p (m n) -> p m n", m=L)
                nc.vector.tensor_tensor(ring[:, t % 4, :, :].rearrange("p l (m n) -> p l m n", m=L),
                                        qv.unsqueeze(2).to_broadcast([P, 2, L, NN]),
                                        kv.unsqueeze(1).to_broadcast([P, 2, L, NN]), ALU.mult).then_inc(prod_ready, 1)

            def weighted_values(blk, t):
                ih = t // LP
                dve.wait_ge(spread_mm, nth(blk, SLOTS, t + 1))
                if t == 0:
                    dve.wait_ge(qkv_ready, nth(blk, 6, 6))
                if t >= 4:
                    dve.wait_ge(o_ready, nth(blk, SLOTS, t - 3))
                ps = psB if t % 2 == 0 else psA
                nc.vector.tensor_tensor(ring[:, t % 4, :, :], ps[:, :, :],
                                        v_sb[:, ih, :].unsqueeze(1).to_broadcast([P, 2, T]), ALU.mult
                                        ).then_inc(av_ready, 1)

            def route(blk, part):
                base = ROUTE_FIRST[part]
                done = [base]

                def link(ins):
                    done[0] += 1
                    ins.then_inc(route_step, 1)
                    dve.wait_ge(route_step, nth(blk, ROUTE_STEPS, done[0]))

                def step(ins):
                    done[0] += 1
                    ins.then_inc(route_step, 1)

                tt = nc.vector.tensor_tensor
                if part == 0:
                    dve.wait_ge(lg_ready, nth(blk, 1, 1))
                    step(tt(lgt[:, :, :], lg[:, :, 0, :], lg[:, :, 1, :], ALU.add))
                elif part == 1:
                    dve.wait_ge(sigexp_ready, nth(blk, 1, 1))
                    link(nc.vector.tensor_scalar_add(sig[:, :, :], sig[:, :, :], 1.0))
                    link(nc.vector.reciprocal(sig[:, :, :], sig[:, :, :]))
                    link(tt(cho[:, :, :], sig[:, :, :], bc_sb[:, :].unsqueeze(1).to_broadcast([P, TT, E]), ALU.add))
                    c4 = cho[:, :, :].rearrange("p t (g x) -> p (t g) x", x=EG)
                    step(tt(pairs[:, :, 0:3], c4[:, :, 0:3], c4[:, :, 1:4], ALU.add))
                    step(tt(pairs[:, :, 3:5], c4[:, :, 0:2], c4[:, :, 2:4], ALU.add))
                    link(tt(pairs[:, :, 5:6], c4[:, :, 0:1], c4[:, :, 3:4], ALU.add))
                    link(nc.vector.reduce_max(gsc[:, :, :].rearrange("p t g -> p (t g)"), pairs[:, :, :], X))
                elif part == 2:
                    other = gsc[:, :, :].unsqueeze(2).to_broadcast([P, TT, G, G])
                    mine = gsc[:, :, :].unsqueeze(3).to_broadcast([P, TT, G, G])
                    step(tt(g_gt[:, :, :, :], other, mine, ALU.is_gt))
                    link(tt(g_ge[:, :, :, :], other, mine, ALU.is_ge))
                    link(tt(g_ge[:, :, :, :], g_ge[:, :, :, :], lower[:, :, :, :], ALU.mult))
                    link(tt(g_gt[:, :, :, :], g_gt[:, :, :, :], g_ge[:, :, :, :], ALU.max))
                    link(nc.vector.reduce_sum(g_rank[:, :], g_gt[:, :, :, :].rearrange("p t g x -> p (t g) x"), X))
                    link(nc.vector.tensor_scalar(g_in[:, :], g_rank[:, :], TOPK_G - 0.5, None, ALU.is_lt))
                elif part == 3:
                    c4 = cho[:, :, :].rearrange("p t (g x) -> p (t g) x", x=EG)
                    step(tt(c4, c4, g_in[:, :].unsqueeze(2).to_broadcast([P, TT * G, EG]), ALU.mult))
                    dve.drain()
                    for j in range(TT):
                        last = nc.vector.max(top8[:, j, :], cho[:, j, :])
                    link(last)
                    kth = top8[:, :, TOPK - 1:TOPK].to_broadcast([P, TT, E])
                    step(tt(e_gt[:, :, :], cho[:, :, :], kth, ALU.is_gt))
                elif part == 4:
                    kth = top8[:, :, TOPK - 1:TOPK].to_broadcast([P, TT, E])
                    link(tt(e_eq[:, :, :], cho[:, :, :], kth, ALU.is_equal))
                    step(nc.vector.reduce_sum(n_gt[:, :], e_gt[:, :, :], X))
                    link(nc.vector.tensor_tensor_scan(e_pre[:, :, :].rearrange("p t e -> p (t e)"),
                                                      not_first[:, :, :].rearrange("p t e -> p (t e)"),
                                                      e_eq[:, :, :].rearrange("p t e -> p (t e)"),
                                                      0.0, ALU.mult, ALU.add))
                    link(tt(e_pre[:, :, :], e_pre[:, :, :], n_gt[:, :].unsqueeze(2).to_broadcast([P, TT, E]), ALU.add))
                    link(nc.vector.tensor_scalar(e_pre[:, :, :], e_pre[:, :, :], TOPK + 0.5, None, ALU.is_lt))
                    link(tt(e_eq[:, :, :], e_eq[:, :, :], e_pre[:, :, :], ALU.mult))
                else:
                    link(tt(e_gt[:, :, :], e_gt[:, :, :], e_eq[:, :, :], ALU.add))
                    link(tt(sig[:, :, :], sig[:, :, :], e_gt[:, :, :], ALU.mult))
                    link(nc.vector.reduce_sum(w_sum[:, :], sig[:, :, :], X))
                    link(nc.vector.tensor_scalar_add(w_sum[:, :], w_sum[:, :], 1e-20))
                    link(nc.vector.reciprocal(w_rec[:, :], w_sum[:, :]))
                    wait(dve, cwT_mm, nth(blk, 1, 0))
                    link(tt(cw[:, :, :], sig[:, :, :], w_rec[:, :].unsqueeze(2).to_broadcast([P, TT, E]), ALU.mult))
                    step(nc.vector.tensor_scalar(cw[:, :, :], cw[:, :, :], ROUTE_SCALE, None, ALU.mult))
                assert done[0] == ROUTE_FIRST[part + 1]

            def attention(blk, h):
                par = blk[1] % 2
                if h in V_PRODUCTS[2:]:
                    product(blk, 2 + V_PRODUCTS[2:].index(h))
                if h == V_MAX:
                    dve.wait_ge(score_mm, nth(blk, SLOTS, SLOTS))
                    nc.vector.reduce_max(s_max[:, :], psA[:, 0, :].rearrange("p (m n) -> p n m", m=L), X
                                         ).then_inc(smax_ready, 1)
                    dve.wait_ge(smax_ready, nth(blk, 1, 1))
                    nc.vector.tensor_tensor(s_sb[:, :, :], psA[:, 0, :].rearrange("p (m n) -> p m n", m=L),
                                            s_max[:, :].unsqueeze(1).to_broadcast([P, L, NN]), ALU.subtract
                                            ).then_inc(ssub_ready, 1)
                if h == V_SUM:
                    dve.wait_ge(exp_ready, nth(blk, 1, 1))
                    nc.vector.reduce_sum(s_sum[:, :], s_sb[:, :, :].rearrange("p m n -> p n m"), X).then_inc(ssum_ready, 1)
                    dve.wait_ge(ssum_ready, nth(blk, 2, 1))
                    nc.vector.reciprocal(s_rec[:, :], s_sum[:, :]).then_inc(ssum_ready, 1)
                    dve.wait_ge(ssum_ready, nth(blk, 2, 2))
                    nc.vector.tensor_tensor(s_sb[:, :, :], s_sb[:, :, :],
                                            s_rec[:, :].unsqueeze(1).to_broadcast([P, L, NN]), ALU.mult
                                            ).then_inc(probs_ready, 1)
                if h == V_PROBS:
                    dve.wait_ge(probs_hi, nth(blk, 1, 1))
                    for ih in range(KH):
                        rows = slice(64 * ih, 64 * ih + 64)
                        last = nc.vector.tensor_tensor(pr[ih][64 - 64 * ih:128 - 64 * ih, :],
                                                       s_sb[rows, :, :].rearrange("p m n -> p (m n)"),
                                                       pr[ih][rows, :].bitcast(f32), ALU.subtract)
                    last.then_inc(probs_lo, 1)
                if V_VALUES <= h < V_VALUES + SLOTS:
                    weighted_values(blk, h - V_VALUES)
                if h in V_OUT:
                    ih = V_OUT.index(h)
                    dve.wait_ge(o_hi, nth(blk, 2, ih + 1))
                    nc.vector.tensor_tensor(xT1[1][:, ih, :], q_sb[:, ih, :], xT1[0][:, ih, :].bitcast(f32),
                                            ALU.subtract).then_inc(o_lo, 1)
                if h == V_H1:
                    dve.wait_ge(outp_mm, nth(blk, 1, 1))
                    dve.wait_ge(xb_ready, nth(blk, 1, 1))
                    dve.wait_ge(h1_free, nth(blk, 1, 1))
                    nc.vector.tensor_tensor(h1[par][:, :, :].rearrange("p j d -> p (j d)"),
                                            psA[:, :, :].rearrange("p a t -> p (a t)"),
                                            xin[par][:, :, :].rearrange("p j d -> p (j d)"), ALU.add
                                            ).then_inc(h1_ready, 1)
                    dve.wait_ge(h1_ready, nth(blk, 1, 1))
                    norm_stats(1, blk, h1[par])
                if h == V_NORM2:
                    normalise(1, blk, h1[par], v_sb)
                if h == V_T2:
                    transposed_lo(1, blk)
                for part, place in enumerate(V_ROUTE):
                    if h == place:
                        route(blk, part)

            def head(blk, h):
                par = blk[1] % 2
                if h == V_STATS1:
                    dve.wait_ge(xin_in[par], turn(blk, 64) + 64)
                    norm_stats(0, blk, xin[par])
                if h == V_NORM1:
                    normalise(0, blk, xin[par], k_sb)
                if h == V_T1:
                    transposed_lo(0, blk)
                if h in V_PRODUCTS[:2]:
                    product(blk, V_PRODUCTS.index(h))

            def block_dve(blk, att, nxt):
                for e in range(X_ALL):
                    if e + 1 < X_ALL:
                        weigh(blk, e + 1)
                    for h, last in ((2 * e, False), (2 * e + 1, True)):
                        if att is not None:
                            attention(att, h)
                        if nxt is not None:
                            head(nxt, h)
                        if last:
                            break
                        if e + 1 < X_ALL:
                            hidden_lo(blk, e + 1)
                        elif att is not None:
                            hidden_lo(att, 0)
                add_experts(blk)

            dve.wait_ge(small_in, 48)
            for h in range(V_T1):
                head((None, 0), h)
            for k in range(PIECES_QKV):
                weight_lo(k)
            for h in range(V_T1, V_PRODUCTS[0]):
                head((None, 0), h)
            for k in range(PIECES_QKV, PIECES_ATT):
                weight_lo(k)
            dve.wait_ge(spread_ready, 1)
            for h in range(V_PRODUCTS[0], HALF):
                head((None, 0), h)
            k = PIECES_ATT
            for h in range(HALF):
                attention((None, 0), h)
                if k < PIECES_ALL:
                    weight_lo(k)
                    k += 1
                head((None, 1), h)
            hidden_lo((None, 0), 0)
            with dve.Fori(0, B // 2 - 1) as i:
                block_dve((i, 0), (i, 1), (i, 2))
                block_dve((i, 1), (i, 2), (i, 3))
            block_dve((None, B - 2), (None, B - 1), None)
            block_dve((None, B - 1), None, None)

        @block.tensor
        def _(pe):
            pe.sem_inc(w2_mm, CREDIT)

            PASSES = [(0, 0), (0, 1), (1, 0)]

            def up(blk, e):
                x = xT2[blk[1] % 2]
                pe.wait_ge(relu_done, nth(blk, X_ALL, e + 1))
                for kh in range(KH):
                    for a, b in PASSES:
                        last = nc.tensor.matmul(psH[:, e % 2, :], W1[a][:, kh, e, :], x[b][:, kh, :],
                                                start=(kh == 0 and (a, b) == PASSES[0]),
                                                stop=(kh == KH - 1 and (a, b) == PASSES[-1]))
                last.then_inc(h_mm, 1)

            def down(blk, e):
                pe.wait_ge(hid_lo, nth(blk, X_ALL, e + 1 + CREDIT))
                if e == 0:
                    pe.wait_ge(y_added, nth(blk, 1, 1))
                for j in range(TT):
                    for a, b in PASSES:
                        last = nc.tensor.matmul(psY[:, j // 2, (j % 2) * D:(j % 2 + 1) * D],
                                                hid[a][:, e % 2, j * P:(j + 1) * P], W2[b][:, e, :],
                                                start=(e == 0 and (a, b) == PASSES[0] and j % 2 == 0),
                                                stop=(e == X_ALL - 1 and (a, b) == PASSES[-1] and j % 2 == 1),
                                                skip_group_check=True)
                last.then_inc(w2_mm, 1)

            def transpose_rows(w, blk):
                pe.wait_ge(xn_ready[w], nth(blk, 1, 1))
                src, ps = (k_sb, psB) if w == 0 else (v_sb, psA)
                if w == 0:
                    wait(pe, av_ready, nth(blk, SLOTS, -1))
                s = src[:, :, :].rearrange("p a t -> p (a t)").rearrange("p (j d) -> p j d", d=D)
                for kh in range(KH):
                    for j in range(TT):
                        last = nc.tensor.transpose(ps[:, kh, j * P:(j + 1) * P], s[:, j, kh * P:(kh + 1) * P],
                                                   ident[:, :])
                last.then_inc(xT_mm[w], 1)

            def qkv(blk, n):
                c, ih = QKV_ORDER[n]
                if n == 0:
                    pe.wait_ge(xT_lo[0], nth(blk, 1, 1))
                if n >= 2:
                    pe.wait_ge(qkv_ready, nth(blk, 6, n - 1))
                for kh in range(KH):
                    for a, b in PASSES:
                        last = nc.tensor.matmul(psB[:, n % 2, :], WQKV[a][:, kh, 2 * c + ih, :], xT1[b][:, kh, :],
                                                start=(kh == 0 and (a, b) == PASSES[0]),
                                                stop=(kh == KH - 1 and (a, b) == PASSES[-1]))
                last.then_inc(qkv_mm, 1)

            def score(blk, t):
                lp, ih = t // KH, t % KH
                pe.wait_ge(prod_ready, nth(blk, SLOTS, t + 1))
                if t == 0:
                    wait(pe, lg_ready, nth(blk, 1, 0))
                for li in range(2):
                    row = 64 * ih + 32 * li
                    last = nc.tensor.matmul(psA[row:row + 32, 0, :], head_sum[:, lp, :], ring[:, t % 4, li, :],
                                            start=(lp == 0), stop=(lp == LP - 1))
                last.then_inc(score_mm, 1)

            def spread_probs(blk, t):
                ih, lp = t // LP, t % LP
                if t == 0:
                    pe.wait_ge(probs_lo, nth(blk, 1, 1))
                    pe.wait_ge(qkv_ready, nth(blk, 6, 6))
                if t == 1:
                    wait(pe, cwT_ready, nth(blk, 1, 0))
                if t >= 2:
                    pe.wait_ge(av_ready, nth(blk, SLOTS, t - 1))
                ps = psB if t % 2 == 0 else psA
                for li in range(2):
                    last = nc.tensor.matmul(ps[:, li, :], spread[:, 2 * lp + li, :], pr[ih][:, :],
                                            start=True, stop=True)
                last.then_inc(spread_mm, 1)

            def out_projection(blk):
                pe.wait_ge(o_lo, nth(blk, 2, 2))
                pe.wait_ge(av_ready, nth(blk, SLOTS, SLOTS))
                for j in range(TT):
                    for ih in range(KH):
                        for a, b in PASSES:
                            last = nc.tensor.matmul(psA[:, j // 2, (j % 2) * D:(j % 2 + 1) * D],
                                                    xT1[a][:, ih, j * P:(j + 1) * P], WO[b][:, ih, :],
                                                    start=(ih == 0 and (a, b) == PASSES[0]),
                                                    stop=(ih == KH - 1 and (a, b) == PASSES[-1]))
                last.then_inc(outp_mm, 1)

            def logits(blk):
                pe.wait_ge(xT_lo[1], nth(blk, 1, 1))
                x = xT2[blk[1] % 2]
                for j in range(TT):
                    for kh in range(KH):
                        for a in range(2):
                            last = nc.tensor.matmul(psA[:, 0, j * 2 * E:(j + 1) * 2 * E],
                                                    x[a][:, kh, j * P:(j + 1) * P],
                                                    WG[:, kh, :, :].rearrange("p a e -> p (a e)"),
                                                    start=(kh == 0 and a == 0), stop=(kh == KH - 1 and a == 1))
                last.then_inc(logit_mm, 1)

            def weights_transpose(blk):
                pe.wait_ge(route_step, nth(blk, ROUTE_STEPS, ROUTE_STEPS))
                for j in range(TT):
                    last = nc.tensor.transpose(psA[0:E, 1, j * P:(j + 1) * P], cw[:, j, :], ident[:, :])
                last.then_inc(cwT_mm, 1)

            def attention(blk, h):
                for t in SCORES.get(h, ()):
                    score(blk, t)
                for t in SPREADS.get(h, ()):
                    spread_probs(blk, t)
                if h == OUT_PROJECTION:
                    out_projection(blk)
                if h == T2:
                    transpose_rows(1, blk)
                if h == LOGITS:
                    logits(blk)
                if h == WEIGHTS:
                    weights_transpose(blk)

            def head(blk, h):
                if h == T1:
                    transpose_rows(0, blk)
                if h in QKV_AT:
                    qkv(blk, QKV_AT.index(h))

            def block_pe(blk, att, nxt):
                for e in range(X_ALL):
                    if e + 2 < X_ALL:
                        up(blk, e + 2)
                    elif att is not None:
                        up(att, e + 2 - X_ALL)
                    for h, last in ((2 * e, False), (2 * e + 1, True)):
                        if att is not None:
                            attention(att, h)
                        if nxt is not None:
                            head(nxt, h)
                        if last:
                            break
                        down(blk, e)

            pe.wait_ge(const_step, CONST_IDENT)
            head((None, 0), T1)
            pe.wait_ge(w_lo, PIECES_QKV)
            for h in range(T1 + 1, HALF):
                head((None, 0), h)
            pe.wait_ge(w_lo, PIECES_ATT)
            pe.wait_ge(const_step, CONST_ALL)
            pe.wait_ge(spread_ready, 1)
            for h in range(HALF):
                attention((None, 0), h)
                head((None, 1), h)
            pe.wait_ge(w_lo, PIECES_ALL)
            up((None, 0), 0)
            up((None, 0), 1)
            with pe.Fori(0, B // 2 - 1) as i:
                block_pe((i, 0), (i, 1), (i, 2))
                block_pe((i, 1), (i, 2), (i, 3))
            block_pe((None, B - 2), (None, B - 1), None)
            block_pe((None, B - 1), None, None)


def kernel(x, L0_tok_weight, L0_attn_qkv_proj, L0_attn_qkv_bias, L0_attn_out_proj, L0_attn_out_bias,
           L0_ffn_Wg, L0_ffn_bias_corr, L0_ffn_W1, L0_ffn_W2, L0_ffn_Ws1, L0_ffn_Ws2):
    import numpy as np
    import concourse.bacc as bacc
    from concourse.bass_utils import run_bass_kernel_spmd

    c = np.ascontiguousarray
    L, N = x.shape
    D = L0_tok_weight.shape[1]
    P, KH = 128, D // 128
    E, I, _ = L0_ffn_W1.shape
    SH = L0_ffn_Ws1.shape[0] // P
    x = np.asarray(x)
    arrays = {
        "ids": c(x.reshape(L // 2, 2, N // 64, 64).transpose(1, 3, 2, 0).reshape(P, -1)),
        "table": c(L0_tok_weight),
        "wqkv_t": c(np.asarray(L0_attn_qkv_proj).reshape(D, 3, KH, P).transpose(3, 2, 1, 0).reshape(P, -1)),
        "bqkv": c(np.asarray(L0_attn_qkv_bias).reshape(KH, P, 3).transpose(1, 2, 0).reshape(P, -1)),
        "wo_t": c(np.asarray(L0_attn_out_proj).reshape(D, KH, P).transpose(2, 1, 0).reshape(P, -1)),
        "bo": c(np.asarray(L0_attn_out_bias).reshape(1, D)),
        "wg_t": c(np.asarray(L0_ffn_Wg).reshape(E, KH, P).transpose(2, 1, 0).reshape(P, -1)),
        "bias_corr": c(np.asarray(L0_ffn_bias_corr).reshape(1, E)),
        "w1_t": c(np.asarray(L0_ffn_W1).reshape(E, I, KH, P).transpose(3, 2, 0, 1).reshape(P, -1)),
        "ws1_t": c(np.asarray(L0_ffn_Ws1).reshape(SH, P, KH, P).transpose(3, 2, 0, 1).reshape(P, -1)),
        "w2_t": c(np.asarray(L0_ffn_W2).transpose(2, 0, 1).reshape(P, -1)),
        "ws2_t": c(np.asarray(L0_ffn_Ws2).reshape(D, SH, P).transpose(2, 1, 0).reshape(P, -1)),
    }
    nc = bacc.Bacc("TRN2", target_bir_lowering=False, num_devices=1)
    args = [nc.dram_tensor(k, a.shape, mybir.dt.from_np(a.dtype), kind="ExternalInput").ap() for k, a in arrays.items()]
    out = nc.dram_tensor("out_0", (L, N, D), mybir.dt.float32, kind="ExternalOutput").ap()
    lm_tower_layer(nc, *args, out)
    r = run_bass_kernel_spmd(nc, [arrays], core_ids=[0])
    return r.results[0]["out_0"]
```

```python
import concourse.bass as bass
from concourse import mybir
from contextlib import ExitStack


def lm_tower_layer(nc: bass.Bass, ids, table, wqkv_t, bqkv, wo_t, bo, wg_t, bias_corr,
                   w1_t, ws1_t, w2_t, ws2_t, out):
    f32 = mybir.dt.float32
    f32r = mybir.dt.float32r
    i32 = mybir.dt.int32
    ALU = mybir.AluOpType
    ACT = mybir.ActivationFunctionType
    X = mybir.AxisListType.X

    P = 128
    VOCAB, D = table.shape
    L, N = out.shape[0], out.shape[1]
    NH = 16
    DH = D // NH
    HH = P // DH
    KH = D // P
    NN = 64
    T = NN * L
    TT = T // P
    B = N // NN
    E = wg_t.shape[1] // KH
    SH = ws1_t.shape[1] // (KH * P)
    X_ALL = E + SH
    G = 4
    EG = E // G
    TOPK_G, TOPK, ROUTE_SCALE = 2, 4, 2.5
    EPS = 1e-5
    ATT_SCALE = float(DH) ** -0.5
    LP = L // 2
    SLOTS = KH * LP
    QN = 2
    QS = E // QN
    HALF = 2 * X_ALL

    def nth(blk, per, k):
        i, off = blk
        return off * per + k if i is None else i * (2 * per) + (off * per + k)

    def turn(blk, per):
        i, off = blk
        return (off // 2) * per if i is None else i * per + (off // 2) * per

    def after(blk, d):
        return (blk[0], blk[1] + d)

    def block_ds(blk):
        return bass.ds(nth(blk, 1, 0), 1)

    def wait(eng, sem, value):
        if not isinstance(value, int) or value > 0:
            eng.wait_ge(sem, value)

    def wait_apart(eng, sem, value):
        value = value if isinstance(value, int) else eng.snap(value)
        eng.wait_ge(sem, 1)
        wait(eng, sem, value)

    ctx = ExitStack()
    with ctx:
        def sb(name, shape, dt=f32):
            return ctx.enter_context(nc.sbuf_tensor(name, shape, dt))

        def pb(name, shape):
            return ctx.enter_context(nc.psum_tensor(name, shape, f32))

        def sem(name):
            return ctx.enter_context(nc.semaphore(name))

        W1 = [sb(f"w1_{p}", [P, KH, X_ALL, P], f32r) for p in ("hi", "lo")]
        W2 = [sb(f"w2_{p}", [P, X_ALL, D], f32r) for p in ("hi", "lo")]
        WQKV = [sb(f"wqkv_{p}", [P, KH, 6, P], f32r) for p in ("hi", "lo")]
        WO = [sb(f"wo_{p}", [P, KH, D], f32r) for p in ("hi", "lo")]
        WG = sb("wg_hi_lo", [P, KH, 2, E], f32r)
        ident = sb("ident", [P, P])
        head_sum = sb("head_sum", [P, 4, 32])
        spread = sb("spread", [P, L, P], f32r)
        bq = sb("bqkv_sb", [P, 6])
        bo_sb = sb("bo_sb", [P, D])
        bc_sb = sb("bias_corr_sb", [P, E])
        half_neg = sb("half_neg", [P, TT])
        lower = sb("lower", [P, TT, G, G])
        not_first = sb("not_first", [P, TT, E])
        idx = sb("idx", [P, B * TT], i32)
        idx_now = sb("idx_now", [P, TT], i32)
        xin = [sb(f"xin{p}", [P, TT, D]) for p in range(2)]
        h1 = [sb(f"h1_{p}", [P, TT, D]) for p in range(2)]
        xT1 = [sb(f"xT1_{p}", [P, KH, T], f32r) for p in ("hi", "lo")]
        xT2 = [[sb(f"xT2_{p}{q}", [P, KH, T], f32r) for p in ("hi", "lo")] for q in range(2)]
        q_sb = sb("q_sb", [P, KH, T])
        k_sb = sb("k_sb", [P, KH, T])
        v_sb = sb("v_sb", [P, KH, T])
        ring = sb("ring", [P, 4, 2, T])
        s_sb = sb("s_sb", [P, L, NN])
        pr = [sb(f"probs{ih}", [P, T], f32r) for ih in range(KH)]
        s_max = sb("s_max", [P, NN])
        s_sum = sb("s_sum", [P, NN])
        s_rec = sb("s_rec", [P, NN])
        stats = [sb(f"stats{w}", [P, TT, 6]) for w in range(2)]
        mv = [sb(f"mv{w}", [P, 4, TT]) for w in range(2)]
        rstd = [sb(f"rstd{w}", [P, TT]) for w in range(2)]
        lg = sb("lg", [P, TT, 2, E])
        lgt = sb("lgt", [P, TT, E])
        sig = sb("sig", [P, TT, E])
        cho = sb("cho", [P, TT, E])
        pairs = sb("pairs", [P, TT * G, 6])
        gsc = sb("gsc", [P, TT, G])
        g_gt = sb("g_gt", [P, TT, G, G])
        g_ge = sb("g_ge", [P, TT, G, G])
        g_rank = sb("g_rank", [P, TT * G])
        top8 = sb("top8", [P, TT, 8])
        e_gt = sb("e_gt", [P, TT, E])
        e_eq = sb("e_eq", [P, TT, E])
        e_pre = sb("e_pre", [P, TT, E])
        n_gt = sb("n_gt", [P, TT])
        w_sum = sb("w_sum", [P, TT])
        w_rec = sb("w_rec", [P, TT])
        cw = sb("cw", [P, TT, E])
        cwT = sb("cwT", [E, T])
        cwB = sb("cwB", [P, 2, QN, T])
        r_sb = sb("r_sb", [P, 2, T])
        p_sb = sb("p_sb", [P, 2, T])
        hid = [sb(f"hid_{p}", [P, 2, T], f32r) for p in ("hi", "lo")]
        stage = [cwB[:, 0, :, :].rearrange("p b t -> p (b t)"), cwB[:, 1, :, :].rearrange("p b t -> p (b t)"),
                 p_sb[:, :, :].rearrange("p b t -> p (b t)"), h1[1][:, :, :].rearrange("p j d -> p (j d)")]
        STAGES = len(stage)

        psH = pb("psH", [P, 2, T])
        psY = pb("psY", [P, 2, T])
        psA = pb("psA", [P, 2, T])
        psB = pb("psB", [P, 2, T])

        cw_dram = nc.dram_tensor("cw_dram", (B, E * T), f32, kind="Internal").ap()

        idx_in = sem("idx_in")
        small_in = sem("small_in")
        w_in = [sem(f"w_in{k}") for k in range(STAGES)]
        w_hi = sem("w_hi")
        w_lo = sem("w_lo")
        const_step = sem("const_step")
        spread_ready = sem("spread_ready")
        idx_now_ready = sem("idx_now_ready")
        xin_in = [sem("xin_in0"), sem("xin_in1")]
        ln_stats = [sem("ln1_stats"), sem("ln2_stats")]
        ln_step = [sem("ln1_step"), sem("ln2_step")]
        ln_rstd = [sem("ln1_rstd"), sem("ln2_rstd")]
        xn_ready = [sem("xn1_ready"), sem("xn2_ready")]
        xT_mm = [sem("xT1_mm"), sem("xT2_mm")]
        xT_hi = [sem("xT1_hi_ready"), sem("xT2_hi_ready")]
        xT_lo = [sem("xT1_lo_ready"), sem("xT2_lo_ready")]
        xb_ready = sem("xb_ready")
        qkv_mm = sem("qkv_mm")
        qkv_ready = sem("qkv_ready")
        prod_ready = [sem("prod_ready_even"), sem("prod_ready_odd")]
        score_mm = sem("score_mm")
        smax_ready = sem("smax_ready")
        ssub_ready = sem("ssub_ready")
        exp_ready = sem("exp_ready")
        ssum_ready = sem("ssum_ready")
        probs_ready = sem("probs_ready")
        probs_hi = sem("probs_hi_ready")
        probs_lo = sem("probs_lo_ready")
        spread_mm = sem("spread_mm")
        av_ready = sem("av_ready")
        sum_step = [sem("sum_step_pool"), sem("sum_step_vector")]
        o_ready = [sem("o_ready_pool"), sem("o_ready_vector")]
        o_hi = sem("o_hi_ready")
        o_lo = sem("o_lo_ready")
        outp_mm = sem("outp_mm")
        h1_ready = sem("h1_ready")
        logit_mm = sem("logit_mm")
        lg_ready = sem("lg_ready")
        route_step = sem("route_step")
        sigexp_ready = sem("sigexp_ready")
        cwT_mm = sem("cwT_mm")
        cwT_ready = sem("cwT_ready")
        cwT_stored = sem("cwT_stored")
        cwB_in = [sem("cwB_in0"), sem("cwB_in1")]
        h_mm = sem("h_mm")
        relu_done = sem("relu_done")
        sq_done = sem("sq_done")
        p_ready = sem("p_ready")
        hid_hi = sem("hid_hi_ready")
        hid_lo = sem("hid_lo_ready")
        w2_mm = sem("w2_mm")
        y_added = sem("y_added")
        out_stored = sem("out_stored")
        h1_free = sem("h1_free")
        CREDIT = 2
        ROUTE_FIRST = [0, 1, 8, 13, 16, 21, 27]
        ROUTE_STEPS = ROUTE_FIRST[-1]
        CONST_IDENT = 3
        CONST_ALL = 15

        def flat(t):
            return t[:, :, :, :].rearrange("p a b c -> p (a b c)") if len(t.shape) == 4 else \
                t[:, :, :].rearrange("p a b -> p (a b)")

        PIECES = []

        def cut(src, dst, base, total, step):
            for at in range(0, total, step):
                n = min(step, total - at)
                PIECES.append((src[:, at:at + n], n, [flat(d)[:, base + at:base + at + n] for d in dst]))

        cut(wqkv_t, WQKV, 0, KH * 6 * P, 768)
        PIECES_QKV = len(PIECES)
        cut(wo_t, WO, 0, KH * D, KH * D)
        for kh in range(KH):
            PIECES.append((wg_t[:, kh * E:(kh + 1) * E], E, [WG[:, kh, s, :] for s in range(2)]))
        PIECES_ATT = len(PIECES)
        for kh in range(KH):
            for src, first, n_e in ((ws1_t, 0, SH), (w1_t, SH, E)):
                cut(src[:, kh * n_e * P:(kh + 1) * n_e * P], W1, (kh * X_ALL + first) * P, n_e * P, 1024)
        cut(ws2_t, W2, 0, SH * D, 1024)
        cut(w2_t, W2, SH * D, E * D, 1024)
        PIECES_ALL = len(PIECES)

        SCORES = [0, 2, 3, 5]
        SPREADS = [10, 10, 11, 12, 13, 14, 15, 16]
        OUT_PROJECTION, T2, LOGITS, WEIGHTS = 21, 26, 28, 34
        A_EXP, A_PROBS, A_OUT, A_T2, A_LOGITS, A_WEIGHTS = 6, 8, (16, 20), 26, 29, 34
        V_PRODUCTS = [33, 0, 1, 3]
        V_MAX, V_SUM, V_PROBS, V_SUMS, V_OUT = 5, 6, 8, (14, 18), (18, 20)
        V_VALUES = [10, 10, 12, 13, 14, 15, 16, 17]
        V_H1, V_NORM2, V_T2 = 23, 25, 27
        V_ROUTE = [29, 29, 30, 31, 32, 33]
        V_STATS1, V_NORM1, V_T1, T1, A_T1 = 4, 9, 24, 19, 24
        QKV_AT = [25, 26, 27, 28, 29, 30]
        A_QKV = [26, 27, 28, 29, 30, 31]

        WEIGHTS_AT = [8, 10, 11, 12, 13, 15, 16, 19, 21, 24, 26]

        QKV_ORDER = [(0, 0), (1, 0), (0, 1), (1, 1), (2, 0), (2, 1)]
        QKV_SB = [q_sb, k_sb, v_sb]

        def product(eng, ns, blk, t):
            lp, ih = t // KH, t % KH
            if lp == 0:
                eng.wait_ge(qkv_ready, nth(blk, 6, 2 * (ih + 1)))
            if t < 4:
                wait_sum(eng, after(blk, -1), t + 4)
            else:
                eng.wait_ge(score_mm, nth(blk, SLOTS, t - 3))
            qv = q_sb[:, ih, 2 * lp * NN:(2 * lp + 2) * NN].rearrange("p (l n) -> p l n", l=2)
            kv = k_sb[:, ih, :].rearrange("p (m n) -> p m n", m=L)
            ns.tensor_tensor(ring[:, t % 4, :, :].rearrange("p l (m n) -> p l m n", m=L),
                             qv.unsqueeze(2).to_broadcast([P, 2, L, NN]),
                             kv.unsqueeze(1).to_broadcast([P, 2, L, NN]), ALU.mult).then_inc(prod_ready[ih], 1)

        def summer(t):
            ih, lp = t // LP, t % LP
            return (1, KH, ih) if lp == LP - 1 else (0, KH * (LP - 1), ih * (LP - 1) + lp)

        def wait_sum(eng, blk, t):
            who, per, k = summer(t)
            wait(eng, o_ready[who], nth(blk, per, k + 1))

        def position_sum(eng, ns, blk, t):
            a = ring[:, t % 4, :, :].rearrange("p l (m n) -> p l m n", m=L)
            ih, lp = t // LP, t % LP
            who, per, k = summer(t)
            eng.wait_ge(av_ready, nth(blk, SLOTS, t + 1))
            ns.tensor_tensor(a[:, :, 0:4, :], a[:, :, 0:4, :], a[:, :, 4:8, :], ALU.add).then_inc(sum_step[who], 1)
            eng.wait_ge(sum_step[who], nth(blk, 2 * per, 2 * k + 1))
            ns.tensor_tensor(a[:, :, 0:2, :], a[:, :, 0:2, :], a[:, :, 2:4, :], ALU.add).then_inc(sum_step[who], 1)
            eng.wait_ge(sum_step[who], nth(blk, 2 * per, 2 * k + 2))
            o = q_sb[:, ih, 2 * lp * NN:(2 * lp + 2) * NN].rearrange("p (l n) -> p l n", l=2)
            ns.tensor_tensor(o, a[:, :, 0, :], a[:, :, 1, :], ALU.add).then_inc(o_ready[who], 1)

        block = ctx.enter_context(nc.Block())

        @block.sync
        def _(sp):
            sp.sem_inc(h1_free, 2)
            sp.dma_start(idx[:, :], ids).then_inc(idx_in, 16)
            for k, (src, n, _dst) in enumerate(PIECES):
                if k >= STAGES:
                    sp.wait_ge(w_lo, k - STAGES + 1)
                sp.dma_start(stage[k % STAGES][:, 0:n], src).then_inc(w_in[k % STAGES], 16)
                if k == PIECES_QKV - 1:
                    sp.dma_start(bq[:, :], bqkv).then_inc(small_in, 16)
                    sp.dma_start(bo_sb[:, :], bo.partition_broadcast(P)).then_inc(small_in, 16)
                    sp.dma_start(bc_sb[:, :], bias_corr.partition_broadcast(P)).then_inc(small_in, 16)
            sp.wait_ge(w_lo, PIECES_ALL)

            out_v = out.rearrange("(j q) (b n) d -> q b n j d", q=2, n=NN)

            def weights_in(blk, g):
                src = cw_dram[block_ds(blk), g * QN * T:(g + 1) * QN * T]
                sp.dma_start(cwB[:, g % 2, :, :].rearrange("p a t -> p (a t)"),
                             src.partition_broadcast(P)).then_inc(cwB_in[g % 2], 16)

            def weights_io(blk):
                sp.wait_ge(cwT_ready, nth(blk, 1, 1))
                sp.dma_start(cw_dram[block_ds(blk), :].rearrange("o (e t) -> (o e) t", t=T),
                             cwT[:, :]).then_inc(cwT_stored, 16)
                sp.wait_ge(cwT_stored, nth(blk, 16, 16))
                weights_in(blk, 0)
                weights_in(blk, 1)

            def block_io(blk, att):
                for g in range(2, QS):
                    sp.wait_ge(p_ready, nth(blk, E, QN * (g - 1)))
                    weights_in(blk, g)
                if att is not None:
                    weights_io(att)
                sp.wait_ge(y_added, nth(blk, 1, 2))
                par = blk[1] % 2
                for q in range(2):
                    sp.dma_start(out_v[q, block_ds(blk), :, :, :].rearrange("o n j d -> (o n) j d"),
                                 h1[par][q * NN:(q + 1) * NN, :, :]).then_inc(out_stored, 16)
                sp.wait_ge(out_stored, nth(blk, 32, 32))
                sp.sem_inc(h1_free, 1)

            weights_io((None, 0))
            with sp.Fori(0, B // 2 - 1) as i:
                block_io((i, 0), (i, 1))
                block_io((i, 1), (i, 2))
            block_io((None, B - 2), (None, B - 1))
            block_io((None, B - 1), None)

        @block.gpsimd
        def _(pool):
            steps = [0]

            def link(ins):
                steps[0] += 1
                ins.then_inc(const_step, 1)
                pool.wait_ge(const_step, steps[0])

            def gather(blk):
                wait(pool, h1_ready, nth(blk, 1, -1))
                nc.gpsimd.tensor_copy(idx_now[:, :], idx[:, bass.ds(nth(blk, TT, 0), TT)]).then_inc(idx_now_ready, 1)
                wait_apart(pool, idx_now_ready, nth(blk, 1, 1) - 2)
                par = blk[1] % 2
                for j in range(TT):
                    nc.gpsimd.indirect_dma_start(xin[par][:, j, :], None, table,
                                                 bass.IndirectOffsetOnAxis(idx_now[:, j:j + 1], 0)
                                                 ).then_inc(xin_in[par], 16)

            def gather_first(b):
                for j in range(TT):
                    nc.gpsimd.indirect_dma_start(xin[b][:, j, :], None, table,
                                                 bass.IndirectOffsetOnAxis(idx[:, b * TT + j:b * TT + j + 1], 0)
                                                 ).then_inc(xin_in[b], 16)

            def rstd_of(w, blk):
                st, m = stats[w], mv[w]
                tt, ts = nc.gpsimd.tensor_tensor, nc.gpsimd.tensor_scalar
                pool.wait_ge(ln_stats[w], nth(blk, 1, 1))
                tt(m[:, 2, :], st[:, :, 2], st[:, :, 5], ALU.add)
                ts(m[:, 0, :], st[:, :, 1], 0.5, None, ALU.mult)
                ts(m[:, 1, :], st[:, :, 4], 0.5, None, ALU.mult).then_inc(ln_step[w], 1)
                pool.wait_ge(ln_step[w], nth(blk, 4, 1))
                tt(m[:, 3, :], m[:, 0, :], m[:, 1, :], ALU.add)
                tt(m[:, 1, :], m[:, 0, :], m[:, 1, :], ALU.subtract)
                ts(m[:, 2, :], m[:, 2, :], 1.0 / D, EPS, ALU.mult, ALU.add).then_inc(ln_step[w], 1)
                pool.wait_ge(ln_step[w], nth(blk, 4, 2))
                tt(m[:, 1, :], m[:, 1, :], m[:, 1, :], ALU.mult).then_inc(ln_step[w], 1)
                pool.wait_ge(ln_step[w], nth(blk, 4, 3))
                tt(m[:, 2, :], m[:, 2, :], m[:, 1, :], ALU.add).then_inc(ln_step[w], 1)
                pool.wait_ge(ln_step[w], nth(blk, 4, 4))
                tt(rstd[w][:, :], m[:, 2, :], half_neg[:, :], ALU.pow).then_inc(ln_rstd[w], 1)

            def bias_in(blk):
                pool.wait_ge(xn_ready[0], nth(blk, 1, 1))
                par = blk[1] % 2
                nc.gpsimd.tensor_tensor(xin[par][:, :, :], xin[par][:, :, :],
                                        bo_sb[:, :].unsqueeze(1).to_broadcast([P, TT, D]), ALU.add).then_inc(xb_ready, 1)

            def main(blk, nxt, far):
                for t in (5, 7):
                    product(pool, nc.gpsimd, blk, t)
                if nxt is not None:
                    rstd_of(0, nxt)
                for t in range(SLOTS):
                    if t % LP < LP - 1:
                        position_sum(pool, nc.gpsimd, blk, t)
                if nxt is not None:
                    bias_in(nxt)
                rstd_of(1, blk)
                if far is not None:
                    gather(far)
                if nxt is not None:
                    product(pool, nc.gpsimd, nxt, 1)
                    product(pool, nc.gpsimd, nxt, 3)

            pool.wait_ge(idx_in, 16)
            gather_first(0)
            link(nc.gpsimd.memset(half_neg[:, :], -0.5))
            link(nc.gpsimd.memset(ident[:, :], 0.0))
            link(nc.gpsimd.affine_select(out=ident[:, :], in_=ident[:, :], compare_op=ALU.not_equal, fill=1.0,
                                         base=0, pattern=[[-1, P]], channel_multiplier=1))
            rstd_of(0, (None, 0))
            gather_first(1)
            link(nc.gpsimd.memset(head_sum[:, :, :], 1.0))
            link(nc.gpsimd.affine_select(out=head_sum[:, :, :], in_=head_sum[:, :, :], compare_op=ALU.is_ge, fill=0.0,
                                         base=0, pattern=[[P, 4], [-DH, 32]], channel_multiplier=1))
            link(nc.gpsimd.affine_select(out=head_sum[:, :, :], in_=head_sum[:, :, :], compare_op=ALU.is_ge, fill=0.0,
                                         base=DH - 1, pattern=[[-P, 4], [DH, 32]], channel_multiplier=-1))
            sp_f = r_sb[:, :, :].rearrange("p b c -> p (b c)")
            link(nc.gpsimd.memset(sp_f, 0.0))
            v = sp_f.rearrange("p (a b h d) -> p a b h d", a=LP, b=2, h=HH)
            for ih in range(KH):
                for b in range(2):
                    link(nc.gpsimd.affine_select(out=v[:, :, b, :, :], in_=v[:, :, b, :, :], compare_op=ALU.not_equal,
                                                 fill=1.0, base=-(64 * ih + 32 * b), channel_multiplier=1,
                                                 pattern=[[-HH, LP], [-1, HH], [0, DH]]))
            link(nc.gpsimd.memset(lower[:, :, :, :], 1.0))
            link(nc.gpsimd.affine_select(out=lower[:, :, :, :], in_=lower[:, :, :, :], compare_op=ALU.is_gt, fill=0.0,
                                         base=0, pattern=[[0, TT], [1, G], [-1, G]], channel_multiplier=0))
            link(nc.gpsimd.memset(not_first[:, :, :], 1.0))
            link(nc.gpsimd.affine_select(out=not_first[:, :, :], in_=not_first[:, :, :], compare_op=ALU.is_gt,
                                         fill=0.0, base=0, pattern=[[0, TT], [1, E]], channel_multiplier=0))
            assert steps[0] == CONST_ALL
            pool.wait_ge(small_in, 48)
            bias_in((None, 0))
            product(pool, nc.gpsimd, (None, 0), 1)
            product(pool, nc.gpsimd, (None, 0), 3)
            main((None, 0), (None, 1), (None, 2))
            with pool.Fori(0, B // 2 - 2) as i:
                main((i, 1), (i, 2), (i, 3))
                main((i, 2), (i, 3), (i, 4))
            main((None, B - 3), (None, B - 2), (None, B - 1))
            main((None, B - 2), (None, B - 1), None)
            main((None, B - 1), None, None)

        @block.scalar
        def _(act):
            act.sem_inc(relu_done, CREDIT)
            act.sem_inc(hid_hi, CREDIT)

            def weight_hi(k):
                src, n, dst = PIECES[k]
                act.wait_ge(w_in[k % STAGES], 16 * (k // STAGES + 1))
                nc.scalar.copy(dst[0], stage[k % STAGES][:, 0:n]).then_inc(w_hi, 1)

            def relu_square(blk, e):
                act.wait_ge(h_mm, nth(blk, X_ALL, e + 1))
                act.wait_ge(hid_lo, nth(blk, X_ALL, e + 1))
                nc.scalar.activation(r_sb[:, e % 2, :], psH[:, e % 2, :], ACT.Relu).then_inc(relu_done, 1)
                act.wait_ge(relu_done, nth(blk, X_ALL, e + 1 + CREDIT))
                nc.scalar.activation(r_sb[:, e % 2, :], r_sb[:, e % 2, :], ACT.Square).then_inc(sq_done, 1)

            def hidden_hi(blk, e):
                if e < SH:
                    act.wait_ge(sq_done, nth(blk, X_ALL, e + 1))
                    src = r_sb
                else:
                    act.wait_ge(p_ready, nth(blk, E, e - SH + 1))
                    src = p_sb
                act.wait_ge(w2_mm, nth(blk, X_ALL, e + 1))
                nc.scalar.copy(hid[0][:, e % 2, :], src[:, e % 2, :]).then_inc(hid_hi, 1)

            def transposed_hi(w, blk):
                act.wait_ge(xT_mm[w], nth(blk, 1, 1))
                if w == 0:
                    wait(act, outp_mm, nth(blk, 1, 0))
                    dst, src = xT1[0], psB
                else:
                    dst, src = xT2[blk[1] % 2][0], psA
                nc.scalar.copy(dst[:, :, :], src[:, :, :]).then_inc(xT_hi[w], 1)

            def qkv_out(blk, n):
                c, ih = QKV_ORDER[n]
                act.wait_ge(qkv_mm, nth(blk, 6, n + 1))
                if n == 0:
                    wait(act, o_lo, nth(blk, 2, 0))
                if n == 4:
                    wait(act, xT_mm[1], nth(blk, 1, 0))
                nc.scalar.activation(QKV_SB[c][:, ih, :], psB[:, n % 2, :], ACT.Identity,
                                     bias=bq[:, 2 * c + ih:2 * c + ih + 1]).then_inc(qkv_ready, 1)

            def weights_out(blk):
                act.wait_ge(cwT_mm, nth(blk, 1, 1))
                nc.scalar.copy(cwT[:, :], psA[0:E, 1, :]).then_inc(cwT_ready, 1)

            def attention(blk, h):
                if h == A_EXP:
                    act.wait_ge(ssub_ready, nth(blk, 1, 1))
                    nc.scalar.activation(s_sb[:, :, :], s_sb[:, :, :], ACT.Exp, scale=ATT_SCALE).then_inc(exp_ready, 1)
                if h == A_PROBS:
                    act.wait_ge(probs_ready, nth(blk, 1, 1))
                    wait(act, spread_mm, nth(blk, SLOTS, 0))
                    for ih in range(KH):
                        rows = slice(64 * ih, 64 * ih + 64)
                        last = nc.scalar.copy(pr[ih][rows, :], s_sb[rows, :, :].rearrange("p m n -> p (m n)"))
                    last.then_inc(probs_hi, 1)
                if h in A_OUT:
                    ih = A_OUT.index(h)
                    wait_sum(act, blk, LP * ih + LP - 2)
                    wait_sum(act, blk, LP * ih + LP - 1)
                    act.wait_ge(qkv_mm, nth(blk, 6, 6))
                    nc.scalar.copy(xT1[0][:, ih, :], q_sb[:, ih, :]).then_inc(o_hi, 1)
                if h == A_T2:
                    transposed_hi(1, blk)
                if h == A_LOGITS:
                    act.wait_ge(logit_mm, nth(blk, 1, 1))
                    wait(act, route_step, nth(blk, ROUTE_STEPS, 1 - ROUTE_STEPS))
                    nc.scalar.copy(lg[:, :, :, :].rearrange("p a b c -> p (a b c)"),
                                   psA[:, 0, 0:TT * 2 * E]).then_inc(lg_ready, 1)
                    act.wait_ge(route_step, nth(blk, ROUTE_STEPS, 1))
                    nc.scalar.activation(sig[:, :, :], lgt[:, :, :], ACT.Exp, scale=-1.0).then_inc(sigexp_ready, 1)
                if h == A_WEIGHTS:
                    weights_out(blk)

            def head(blk, h):
                if h == A_T1:
                    transposed_hi(0, blk)
                for n, place in enumerate(A_QKV):
                    if h == place:
                        qkv_out(blk, n)

            def block_act(blk, att, nxt):
                for e in range(X_ALL):
                    if e + 1 < X_ALL:
                        relu_square(blk, e + 1)
                    elif att is not None:
                        relu_square(att, 0)
                    for h, last in ((2 * e, False), (2 * e + 1, True)):
                        if att is not None:
                            attention(att, h)
                        if nxt is not None:
                            head(nxt, h)
                        if last:
                            break
                        if e + 1 < X_ALL:
                            hidden_hi(blk, e + 1)
                        elif att is not None:
                            hidden_hi(att, 0)

            for k in range(PIECES_QKV):
                weight_hi(k)
            act.wait_ge(small_in, 48)
            act.wait_ge(const_step, CONST_IDENT)
            for h in range(HALF):
                head((None, 0), h)
            for k in range(PIECES_QKV, PIECES_ATT):
                weight_hi(k)
            act.wait_ge(const_step, CONST_ALL)
            nc.scalar.copy(spread[:, :, :].rearrange("p a b -> p (a b)"),
                           r_sb[:, :, :].rearrange("p b c -> p (b c)")).then_inc(spread_ready, 1)
            for h in range(HALF):
                attention((None, 0), h)
                if h in WEIGHTS_AT:
                    weight_hi(PIECES_ATT + WEIGHTS_AT.index(h))
                head((None, 1), h)
                if h == LOGITS + 3:
                    relu_square((None, 0), 0)
                    hidden_hi((None, 0), 0)
            with act.Fori(0, B // 2 - 1) as i:
                block_act((i, 0), (i, 1), (i, 2))
                block_act((i, 1), (i, 2), (i, 3))
            block_act((None, B - 2), (None, B - 1), None)
            block_act((None, B - 1), None, None)

        @block.vector
        def _(dve):
            dve.sem_inc(hid_lo, CREDIT)
            dve.sem_inc(y_added, 1)

            def weight_lo(k):
                src, n, dst = PIECES[k]
                dve.wait_ge(w_hi, k + 1)
                nc.vector.tensor_tensor(dst[1], stage[k % STAGES][:, 0:n], dst[0].bitcast(f32), ALU.subtract).then_inc(w_lo, 1)

            def weigh(blk, e):
                if e < SH:
                    return
                r = e - SH
                dve.wait_ge(sq_done, nth(blk, X_ALL, e + 1))
                if r % QN == 0:
                    g = r // QN
                    dve.wait_ge(cwB_in[g % 2], nth(blk, 16 * QS // 2, 16 * (g // 2 + 1)))
                dve.wait_ge(hid_hi, nth(blk, X_ALL, e + 1))
                nc.vector.tensor_tensor(p_sb[:, e % 2, :], r_sb[:, e % 2, :],
                                        cwB[:, (r // QN) % 2, r % QN, :], ALU.mult).then_inc(p_ready, 1)

            def hidden_lo(blk, e):
                src = r_sb if e < SH else p_sb
                dve.wait_ge(hid_hi, nth(blk, X_ALL, e + 1 + CREDIT))
                nc.vector.tensor_tensor(hid[1][:, e % 2, :], src[:, e % 2, :],
                                        hid[0][:, e % 2, :].bitcast(f32), ALU.subtract).then_inc(hid_lo, 1)

            def add_experts(blk):
                par = blk[1] % 2
                dve.wait_ge(w2_mm, nth(blk, X_ALL, X_ALL + CREDIT))
                nc.vector.tensor_tensor(h1[par][:, :, :].rearrange("p j d -> p (j d)"),
                                        psY[:, :, :].rearrange("p a t -> p (a t)"),
                                        h1[par][:, :, :].rearrange("p j d -> p (j d)"), ALU.add).then_inc(y_added, 1)

            def norm_stats(w, blk, src):
                for j in range(TT):
                    last = nc.vector.bn_stats(stats[w][:, j, :], src[:, j, :])
                last.then_inc(ln_stats[w], 1)

            def normalise(w, blk, src, dst):
                dve.wait_ge(ln_rstd[w], nth(blk, 1, 1))
                d = dst[:, :, :].rearrange("p a t -> p (a t)").rearrange("p (j d) -> p j d", d=D)
                for j in range(TT):
                    last = nc.vector.tensor_scalar(d[:, j, :], src[:, j, :], mv[w][:, 3, j:j + 1], rstd[w][:, j:j + 1],
                                                   ALU.subtract, ALU.mult)
                last.then_inc(xn_ready[w], 1)

            def transposed_lo(w, blk):
                src, dst = (psB, xT1) if w == 0 else (psA, xT2[blk[1] % 2])
                dve.wait_ge(xT_hi[w], nth(blk, 1, 1))
                nc.vector.tensor_tensor(dst[1][:, :, :], src[:, :, :], dst[0][:, :, :].bitcast(f32),
                                        ALU.subtract).then_inc(xT_lo[w], 1)

            def weighted_values(blk, t):
                ih = t // LP
                dve.wait_ge(spread_mm, nth(blk, SLOTS, t + 1))
                if t == 0:
                    dve.wait_ge(qkv_ready, nth(blk, 6, 6))
                if t >= 4:
                    wait_sum(dve, blk, t - 4)
                ps = psB if t % 2 == 0 else psA
                nc.vector.tensor_tensor(ring[:, t % 4, :, :], ps[:, :, :],
                                        v_sb[:, ih, :].unsqueeze(1).to_broadcast([P, 2, T]), ALU.mult
                                        ).then_inc(av_ready, 1)

            def route(blk, part):
                base = ROUTE_FIRST[part]
                done = [base]

                def link(ins):
                    done[0] += 1
                    ins.then_inc(route_step, 1)
                    dve.wait_ge(route_step, nth(blk, ROUTE_STEPS, done[0]))

                def step(ins):
                    done[0] += 1
                    ins.then_inc(route_step, 1)

                tt = nc.vector.tensor_tensor
                if part == 0:
                    dve.wait_ge(lg_ready, nth(blk, 1, 1))
                    step(tt(lgt[:, :, :], lg[:, :, 0, :], lg[:, :, 1, :], ALU.add))
                elif part == 1:
                    dve.wait_ge(sigexp_ready, nth(blk, 1, 1))
                    link(nc.vector.tensor_scalar_add(sig[:, :, :], sig[:, :, :], 1.0))
                    link(nc.vector.reciprocal(sig[:, :, :], sig[:, :, :]))
                    link(tt(cho[:, :, :], sig[:, :, :], bc_sb[:, :].unsqueeze(1).to_broadcast([P, TT, E]), ALU.add))
                    c4 = cho[:, :, :].rearrange("p t (g x) -> p (t g) x", x=EG)
                    step(tt(pairs[:, :, 0:3], c4[:, :, 0:3], c4[:, :, 1:4], ALU.add))
                    step(tt(pairs[:, :, 3:5], c4[:, :, 0:2], c4[:, :, 2:4], ALU.add))
                    link(tt(pairs[:, :, 5:6], c4[:, :, 0:1], c4[:, :, 3:4], ALU.add))
                    link(nc.vector.reduce_max(gsc[:, :, :].rearrange("p t g -> p (t g)"), pairs[:, :, :], X))
                elif part == 2:
                    other = gsc[:, :, :].unsqueeze(2).to_broadcast([P, TT, G, G])
                    mine = gsc[:, :, :].unsqueeze(3).to_broadcast([P, TT, G, G])
                    step(tt(g_gt[:, :, :, :], other, mine, ALU.is_gt))
                    link(tt(g_ge[:, :, :, :], other, mine, ALU.is_ge))
                    link(tt(g_ge[:, :, :, :], g_ge[:, :, :, :], lower[:, :, :, :], ALU.mult))
                    link(tt(g_gt[:, :, :, :], g_gt[:, :, :, :], g_ge[:, :, :, :], ALU.max))
                    link(nc.vector.reduce_sum(g_rank[:, :], g_gt[:, :, :, :].rearrange("p t g x -> p (t g) x"), X))
                elif part == 3:
                    c4 = cho[:, :, :].rearrange("p t (g x) -> p (t g) x", x=EG)
                    step(nc.vector.scalar_tensor_tensor(c4, g_rank[:, :].unsqueeze(2).to_broadcast([P, TT * G, EG]),
                                                        TOPK_G - 0.5, c4, ALU.is_lt, ALU.mult))
                    dve.drain()
                    for j in range(TT):
                        last = nc.vector.max(top8[:, j, :], cho[:, j, :])
                    link(last)
                    kth = top8[:, :, TOPK - 1:TOPK].to_broadcast([P, TT, E])
                    step(tt(e_gt[:, :, :], cho[:, :, :], kth, ALU.is_gt))
                elif part == 4:
                    kth = top8[:, :, TOPK - 1:TOPK].to_broadcast([P, TT, E])
                    link(tt(e_eq[:, :, :], cho[:, :, :], kth, ALU.is_equal))
                    step(nc.vector.reduce_sum(n_gt[:, :], e_gt[:, :, :], X))
                    link(nc.vector.tensor_tensor_scan(e_pre[:, :, :].rearrange("p t e -> p (t e)"),
                                                      not_first[:, :, :].rearrange("p t e -> p (t e)"),
                                                      e_eq[:, :, :].rearrange("p t e -> p (t e)"),
                                                      0.0, ALU.mult, ALU.add))
                    link(tt(e_pre[:, :, :], e_pre[:, :, :], n_gt[:, :].unsqueeze(2).to_broadcast([P, TT, E]), ALU.add))
                    link(nc.vector.scalar_tensor_tensor(e_eq[:, :, :], e_pre[:, :, :], TOPK + 0.5, e_eq[:, :, :],
                                                        ALU.is_lt, ALU.mult))
                else:
                    link(tt(e_gt[:, :, :], e_gt[:, :, :], e_eq[:, :, :], ALU.add))
                    link(tt(sig[:, :, :], sig[:, :, :], e_gt[:, :, :], ALU.mult))
                    link(nc.vector.reduce_sum(w_sum[:, :], sig[:, :, :], X))
                    link(nc.vector.tensor_scalar_add(w_sum[:, :], w_sum[:, :], 1e-20))
                    link(nc.vector.reciprocal(w_rec[:, :], w_sum[:, :]))
                    wait(dve, cwT_mm, nth(blk, 1, 0))
                    step(nc.vector.scalar_tensor_tensor(cw[:, :, :], sig[:, :, :], ROUTE_SCALE,
                                                        w_rec[:, :].unsqueeze(2).to_broadcast([P, TT, E]),
                                                        ALU.mult, ALU.mult))
                assert done[0] == ROUTE_FIRST[part + 1]

            def attention(blk, h):
                par = blk[1] % 2
                if h in V_PRODUCTS[1:]:
                    product(dve, nc.vector, blk, 2 * V_PRODUCTS.index(h))
                if h == V_MAX:
                    dve.wait_ge(score_mm, nth(blk, SLOTS, SLOTS))
                    nc.vector.reduce_max(s_max[:, :], psA[:, 0, :].rearrange("p (m n) -> p n m", m=L), X
                                         ).then_inc(smax_ready, 1)
                    dve.wait_ge(smax_ready, nth(blk, 1, 1))
                    nc.vector.tensor_tensor(s_sb[:, :, :], psA[:, 0, :].rearrange("p (m n) -> p m n", m=L),
                                            s_max[:, :].unsqueeze(1).to_broadcast([P, L, NN]), ALU.subtract
                                            ).then_inc(ssub_ready, 1)
                if h == V_SUM:
                    dve.wait_ge(exp_ready, nth(blk, 1, 1))
                    nc.vector.reduce_sum(s_sum[:, :], s_sb[:, :, :].rearrange("p m n -> p n m"), X).then_inc(ssum_ready, 1)
                    dve.wait_ge(ssum_ready, nth(blk, 2, 1))
                    nc.vector.reciprocal(s_rec[:, :], s_sum[:, :]).then_inc(ssum_ready, 1)
                    dve.wait_ge(ssum_ready, nth(blk, 2, 2))
                    nc.vector.tensor_tensor(s_sb[:, :, :], s_sb[:, :, :],
                                            s_rec[:, :].unsqueeze(1).to_broadcast([P, L, NN]), ALU.mult
                                            ).then_inc(probs_ready, 1)
                if h == V_PROBS:
                    dve.wait_ge(probs_hi, nth(blk, 1, 1))
                    for ih in range(KH):
                        rows = slice(64 * ih, 64 * ih + 64)
                        last = nc.vector.tensor_tensor(pr[ih][64 - 64 * ih:128 - 64 * ih, :],
                                                       s_sb[rows, :, :].rearrange("p m n -> p (m n)"),
                                                       pr[ih][rows, :].bitcast(f32), ALU.subtract)
                    last.then_inc(probs_lo, 1)
                for t, place in enumerate(V_VALUES):
                    if h == place:
                        weighted_values(blk, t)
                if h in V_SUMS:
                    position_sum(dve, nc.vector, blk, LP * V_SUMS.index(h) + LP - 1)
                if h in V_OUT:
                    ih = V_OUT.index(h)
                    dve.wait_ge(o_hi, nth(blk, 2, ih + 1))
                    nc.vector.tensor_tensor(xT1[1][:, ih, :], q_sb[:, ih, :], xT1[0][:, ih, :].bitcast(f32),
                                            ALU.subtract).then_inc(o_lo, 1)
                if h == V_H1:
                    dve.wait_ge(outp_mm, nth(blk, 1, 1))
                    dve.wait_ge(xb_ready, nth(blk, 1, 1))
                    dve.wait_ge(h1_free, nth(blk, 1, 1))
                    nc.vector.tensor_tensor(h1[par][:, :, :].rearrange("p j d -> p (j d)"),
                                            psA[:, :, :].rearrange("p a t -> p (a t)"),
                                            xin[par][:, :, :].rearrange("p j d -> p (j d)"), ALU.add
                                            ).then_inc(h1_ready, 1)
                    dve.wait_ge(h1_ready, nth(blk, 1, 1))
                    norm_stats(1, blk, h1[par])
                if h == V_NORM2:
                    normalise(1, blk, h1[par], v_sb)
                if h == V_T2:
                    transposed_lo(1, blk)
                for part, place in enumerate(V_ROUTE):
                    if h == place:
                        route(blk, part)

            def head(blk, h):
                par = blk[1] % 2
                if h == V_STATS1:
                    dve.wait_ge(xin_in[par], turn(blk, 64) + 64)
                    norm_stats(0, blk, xin[par])
                if h == V_NORM1:
                    normalise(0, blk, xin[par], k_sb)
                if h == V_T1:
                    transposed_lo(0, blk)
                if h == V_PRODUCTS[0]:
                    product(dve, nc.vector, blk, 0)

            def block_dve(blk, att, nxt):
                for e in range(X_ALL):
                    if e + 1 < X_ALL:
                        weigh(blk, e + 1)
                    for h, last in ((2 * e, False), (2 * e + 1, True)):
                        if att is not None:
                            attention(att, h)
                        if nxt is not None:
                            head(nxt, h)
                        if last:
                            break
                        if e + 1 < X_ALL:
                            hidden_lo(blk, e + 1)
                        elif att is not None:
                            hidden_lo(att, 0)
                add_experts(blk)

            for h in range(V_T1):
                head((None, 0), h)
            for k in range(PIECES_QKV):
                weight_lo(k)
            dve.wait_ge(small_in, 48)
            for h in range(V_T1, HALF):
                head((None, 0), h)
            for h in range(HALF):
                attention((None, 0), h)
                if h == V_MAX:
                    for k in range(PIECES_QKV, PIECES_ATT):
                        weight_lo(k)
                if h in WEIGHTS_AT:
                    weight_lo(PIECES_ATT + WEIGHTS_AT.index(h))
                head((None, 1), h)
            hidden_lo((None, 0), 0)
            with dve.Fori(0, B // 2 - 1) as i:
                block_dve((i, 0), (i, 1), (i, 2))
                block_dve((i, 1), (i, 2), (i, 3))
            block_dve((None, B - 2), (None, B - 1), None)
            block_dve((None, B - 1), None, None)

        @block.tensor
        def _(pe):
            pe.sem_inc(w2_mm, CREDIT)

            PASSES = [(0, 0), (0, 1), (1, 0)]

            def up(blk, e):
                x = xT2[blk[1] % 2]
                pe.wait_ge(relu_done, nth(blk, X_ALL, e + 1))
                for kh in range(KH):
                    for a, b in PASSES:
                        last = nc.tensor.matmul(psH[:, e % 2, :], W1[a][:, kh, e, :], x[b][:, kh, :],
                                                start=(kh == 0 and (a, b) == PASSES[0]),
                                                stop=(kh == KH - 1 and (a, b) == PASSES[-1]))
                last.then_inc(h_mm, 1)

            def down(blk, e):
                pe.wait_ge(hid_lo, nth(blk, X_ALL, e + 1 + CREDIT))
                if e == 0:
                    pe.wait_ge(y_added, nth(blk, 1, 1))
                for j in range(TT):
                    for a, b in PASSES:
                        last = nc.tensor.matmul(psY[:, j // 2, (j % 2) * D:(j % 2 + 1) * D],
                                                hid[a][:, e % 2, j * P:(j + 1) * P], W2[b][:, e, :],
                                                start=(e == 0 and (a, b) == PASSES[0] and j % 2 == 0),
                                                stop=(e == X_ALL - 1 and (a, b) == PASSES[-1] and j % 2 == 1),
                                                skip_group_check=True)
                last.then_inc(w2_mm, 1)

            def transpose_rows(w, blk):
                pe.wait_ge(xn_ready[w], nth(blk, 1, 1))
                src, ps = (k_sb, psB) if w == 0 else (v_sb, psA)
                if w == 0:
                    wait(pe, av_ready, nth(blk, SLOTS, -1))
                s = src[:, :, :].rearrange("p a t -> p (a t)").rearrange("p (j d) -> p j d", d=D)
                for kh in range(KH):
                    for j in range(TT):
                        last = nc.tensor.transpose(ps[:, kh, j * P:(j + 1) * P], s[:, j, kh * P:(kh + 1) * P],
                                                   ident[:, :])
                last.then_inc(xT_mm[w], 1)

            def qkv(blk, n):
                c, ih = QKV_ORDER[n]
                if n == 0:
                    pe.wait_ge(xT_lo[0], nth(blk, 1, 1))
                if n >= 2:
                    pe.wait_ge(qkv_ready, nth(blk, 6, n - 1))
                for kh in range(KH):
                    for a, b in PASSES:
                        last = nc.tensor.matmul(psB[:, n % 2, :], WQKV[a][:, kh, 2 * c + ih, :], xT1[b][:, kh, :],
                                                start=(kh == 0 and (a, b) == PASSES[0]),
                                                stop=(kh == KH - 1 and (a, b) == PASSES[-1]))
                last.then_inc(qkv_mm, 1)

            def score(blk, t):
                lp, ih = t // KH, t % KH
                pe.wait_ge(prod_ready[ih], nth(blk, LP, lp + 1))
                if t == 0:
                    wait(pe, lg_ready, nth(blk, 1, 0))
                for li in range(2):
                    row = 64 * ih + 32 * li
                    last = nc.tensor.matmul(psA[row:row + 32, 0, :], head_sum[:, lp, :], ring[:, t % 4, li, :],
                                            start=(lp == 0), stop=(lp == LP - 1))
                last.then_inc(score_mm, 1)

            def spread_probs(blk, t):
                ih, lp = t // LP, t % LP
                if t == 0:
                    pe.wait_ge(probs_lo, nth(blk, 1, 1))
                    pe.wait_ge(qkv_ready, nth(blk, 6, 6))
                if t == 1:
                    wait(pe, cwT_ready, nth(blk, 1, 0))
                if t >= 2:
                    pe.wait_ge(av_ready, nth(blk, SLOTS, t - 1))
                ps = psB if t % 2 == 0 else psA
                for li in range(2):
                    last = nc.tensor.matmul(ps[:, li, :], spread[:, 2 * lp + li, :], pr[ih][:, :],
                                            start=True, stop=True)
                last.then_inc(spread_mm, 1)

            def out_projection(blk):
                pe.wait_ge(o_lo, nth(blk, 2, 2))
                pe.wait_ge(av_ready, nth(blk, SLOTS, SLOTS))
                for j in range(TT):
                    for ih in range(KH):
                        for a, b in PASSES:
                            last = nc.tensor.matmul(psA[:, j // 2, (j % 2) * D:(j % 2 + 1) * D],
                                                    xT1[a][:, ih, j * P:(j + 1) * P], WO[b][:, ih, :],
                                                    start=(ih == 0 and (a, b) == PASSES[0]),
                                                    stop=(ih == KH - 1 and (a, b) == PASSES[-1]))
                last.then_inc(outp_mm, 1)

            def logits(blk):
                pe.wait_ge(xT_lo[1], nth(blk, 1, 1))
                x = xT2[blk[1] % 2]
                for j in range(TT):
                    for kh in range(KH):
                        for a in range(2):
                            last = nc.tensor.matmul(psA[:, 0, j * 2 * E:(j + 1) * 2 * E],
                                                    x[a][:, kh, j * P:(j + 1) * P],
                                                    WG[:, kh, :, :].rearrange("p a e -> p (a e)"),
                                                    start=(kh == 0 and a == 0), stop=(kh == KH - 1 and a == 1))
                last.then_inc(logit_mm, 1)

            def weights_transpose(blk):
                pe.wait_ge(route_step, nth(blk, ROUTE_STEPS, ROUTE_STEPS))
                for j in range(TT):
                    last = nc.tensor.transpose(psA[0:E, 1, j * P:(j + 1) * P], cw[:, j, :], ident[:, :])
                last.then_inc(cwT_mm, 1)

            def attention(blk, h):
                for lp, place in enumerate(SCORES):
                    if h == place:
                        score(blk, KH * lp)
                        score(blk, KH * lp + 1)
                for t, place in enumerate(SPREADS):
                    if h == place:
                        spread_probs(blk, t)
                if h == OUT_PROJECTION:
                    out_projection(blk)
                if h == T2:
                    transpose_rows(1, blk)
                if h == LOGITS:
                    logits(blk)
                if h == WEIGHTS:
                    weights_transpose(blk)

            def head(blk, h):
                if h == T1:
                    transpose_rows(0, blk)
                for n, place in enumerate(QKV_AT):
                    if h == place:
                        qkv(blk, n)

            def block_pe(blk, att, nxt):
                for e in range(X_ALL):
                    if e + 2 < X_ALL:
                        up(blk, e + 2)
                    elif att is not None:
                        up(att, e + 2 - X_ALL)
                    for h, last in ((2 * e, False), (2 * e + 1, True)):
                        if att is not None:
                            attention(att, h)
                        if nxt is not None:
                            head(nxt, h)
                        if last:
                            break
                        down(blk, e)

            pe.wait_ge(const_step, CONST_IDENT)
            head((None, 0), T1)
            pe.wait_ge(w_lo, PIECES_QKV)
            for h in range(T1 + 1, HALF):
                head((None, 0), h)
            pe.wait_ge(const_step, CONST_ALL)
            for h in range(HALF):
                if h == 9:
                    pe.wait_ge(spread_ready, 1)
                if h == OUT_PROJECTION:
                    pe.wait_ge(w_lo, PIECES_ATT)
                attention((None, 0), h)
                head((None, 1), h)
                if h == LOGITS + 2:
                    pe.wait_ge(w_lo, PIECES_ALL)
                    up((None, 0), 0)
                    up((None, 0), 1)
            with pe.Fori(0, B // 2 - 1) as i:
                block_pe((i, 0), (i, 1), (i, 2))
                block_pe((i, 1), (i, 2), (i, 3))
            block_pe((None, B - 2), (None, B - 1), None)
            block_pe((None, B - 1), None, None)


def kernel(x, L0_tok_weight, L0_attn_qkv_proj, L0_attn_qkv_bias, L0_attn_out_proj, L0_attn_out_bias,
           L0_ffn_Wg, L0_ffn_bias_corr, L0_ffn_W1, L0_ffn_W2, L0_ffn_Ws1, L0_ffn_Ws2):
    import numpy as np
    import concourse.bacc as bacc
    from concourse.bass_utils import run_bass_kernel_spmd

    c = np.ascontiguousarray
    L, N = x.shape
    D = L0_tok_weight.shape[1]
    P, KH = 128, D // 128
    E, I, _ = L0_ffn_W1.shape
    SH = L0_ffn_Ws1.shape[0] // P
    x = np.asarray(x)
    arrays = {
        "ids": c(x.reshape(L // 2, 2, N // 64, 64).transpose(1, 3, 2, 0).reshape(P, -1)),
        "table": c(L0_tok_weight),
        "wqkv_t": c(np.asarray(L0_attn_qkv_proj).reshape(D, 3, KH, P).transpose(3, 2, 1, 0).reshape(P, -1)),
        "bqkv": c(np.asarray(L0_attn_qkv_bias).reshape(KH, P, 3).transpose(1, 2, 0).reshape(P, -1)),
        "wo_t": c(np.asarray(L0_attn_out_proj).reshape(D, KH, P).transpose(2, 1, 0).reshape(P, -1)),
        "bo": c(np.asarray(L0_attn_out_bias).reshape(1, D)),
        "wg_t": c(np.asarray(L0_ffn_Wg).reshape(E, KH, P).transpose(2, 1, 0).reshape(P, -1)),
        "bias_corr": c(np.asarray(L0_ffn_bias_corr).reshape(1, E)),
        "w1_t": c(np.asarray(L0_ffn_W1).reshape(E, I, KH, P).transpose(3, 2, 0, 1).reshape(P, -1)),
        "ws1_t": c(np.asarray(L0_ffn_Ws1).reshape(SH, P, KH, P).transpose(3, 2, 0, 1).reshape(P, -1)),
        "w2_t": c(np.asarray(L0_ffn_W2).transpose(2, 0, 1).reshape(P, -1)),
        "ws2_t": c(np.asarray(L0_ffn_Ws2).reshape(D, SH, P).transpose(2, 1, 0).reshape(P, -1)),
    }
    nc = bacc.Bacc("TRN2", target_bir_lowering=False, num_devices=1)
    args = [nc.dram_tensor(k, a.shape, mybir.dt.from_np(a.dtype), kind="ExternalInput").ap() for k, a in arrays.items()]
    out = nc.dram_tensor("out_0", (L, N, D), mybir.dt.float32, kind="ExternalOutput").ap()
    lm_tower_layer(nc, *args, out)
    r = run_bass_kernel_spmd(nc, [arrays], core_ids=[0])
    return r.results[0]["out_0"]
```
